# Optimizing a Trainium2 kernel written in Bass

```python
import numpy as np
import jax
import jax.numpy as jnp

def _softmax(x, axis=-1):
    return jax.nn.softmax(x, axis=axis)

def _gelu(x):
    return jax.nn.gelu(x, approximate=True)

def _silu(x):
    return jax.nn.silu(x)

def _sigmoid(x):
    return jax.nn.sigmoid(x)

def _layernorm(x, axis=-1, eps=1e-05):
    m = jnp.mean(x, axis=axis, keepdims=True)
    v = jnp.var(x, axis=axis, keepdims=True)
    return (x - m) / jnp.sqrt(v + eps)

def _scatter_add(tgt, idx, src, axis=0):
    return tgt.at[idx].add(src)

def _segment_sum(src, seg, n):
    return jax.ops.segment_sum(src, seg, n)
kernel_name = 'mk_adj_resnorm_d2_adj_r2_1b30f1'

def setup_inputs(seed: int=0):
    np.random.seed(seed)
    _w = jnp.asarray

    def _rec_inputs():
        import jax
        import jax.numpy as jnp
        _gk = jax.random.key(seed)
        x = 7.22e-05 + 1 * jax.random.normal(jax.random.fold_in(_gk, 1), (32, 256, 256), jnp.float32)
        _a = jax.random.bernoulli(jax.random.fold_in(_gk, 2), 0.0078125, (32, 256, 256))
        _a = jnp.logical_or(_a, jnp.swapaxes(_a, -1, -2))
        _a = jnp.logical_or(_a, jnp.eye(256, dtype=bool))
        _af = _a.astype(jnp.float32)
        _af = _af * jax.random.uniform(jax.random.fold_in(_gk, 3), (32, 256, 256), jnp.float32, 0.05, 1)
        adj = _af
        return (x, adj)
    x, adj = _rec_inputs()

    def _L0_gnn_setup():
        import jax, jax.numpy as jnp
        import numpy as np
        EPS_LN = 1e-05

        def hypergraph_conv(x, adj, W, b):
            N, C, _ = adj.shape
            H = (adj != 0).astype(x.dtype)
            w = adj.reshape(N, -1)[:, :C]
            xw = jnp.einsum('ncd,hd->nch', x, W)
            Dn = jnp.einsum('nce,ne->nc', H, w)
            Dn = jnp.where(Dn > 0, 1.0 / Dn, 0.0)
            Be = H.sum(axis=1)
            Be = jnp.where(Be > 0, 1.0 / Be, 0.0)
            m = Be[:, :, None] * jnp.einsum('nce,nch->neh', H, xw)
            out = Dn[:, :, None] * jnp.einsum('nce,neh->nch', H, m)
            return out + b

        def layer_norm(x, g, b):
            mu = jnp.mean(x, axis=-1, keepdims=True)
            var = jnp.var(x, axis=-1, keepdims=True)
            return (x - mu) * jax.lax.rsqrt(var + EPS_LN) * g + b
        key = jax.random.key(seed)
        ks = jax.random.split(key, 4)
        N, C, Din, Dh, Dout = (16, 512, 256, 512, 256)
        x = jax.random.normal(ks[0], (N, C, Din), dtype=jnp.float32)
        adj = jax.random.uniform(ks[1], (N, C, C), dtype=jnp.float32, minval=0.1, maxval=1.0)
        W1 = jax.random.normal(ks[2], (Dh, Din), dtype=jnp.float32) * (1.0 / np.sqrt(Din))
        b1 = jnp.zeros((Dh,), dtype=jnp.float32)
        gamma = jnp.ones((Dh,), dtype=jnp.float32)
        beta = jnp.zeros((Dh,), dtype=jnp.float32)
        W2 = jax.random.normal(ks[3], (Dout, Dh), dtype=jnp.float32) * (1.0 / np.sqrt(Dh))
        b2 = jnp.zeros((Dout,), dtype=jnp.float32)
        return {'x': x, 'adj': adj, 'W1': W1, 'b1': b1, 'gamma': gamma, 'beta': beta, 'W2': W2, 'b2': b2}
    _L0_gnn_all = _L0_gnn_setup()
    _L0_gnn_in = {k: v for k, v in _L0_gnn_all.items() if k in ('W1', 'b1', 'gamma', 'beta', 'W2', 'b2')}
    del _L0_gnn_all

    def _L1_gnn_setup():
        import jax, jax.numpy as jnp
        import numpy as np
        B, N, DIN, DOUT = (8, 1024, 256, 256)
        EDGE_P = 0.01

        def _gcn_norm(adj):
            A = (adj != 0).astype(adj.dtype)
            eye = jnp.eye(A.shape[-1], dtype=A.dtype)
            A = jnp.maximum(A, eye)
            deg = A.sum(axis=-1)
            dinv = jnp.where(deg > 0, jax.lax.rsqrt(deg), 0.0)
            return dinv[..., :, None] * A * dinv[..., None, :]
        key = jax.random.key(seed)
        k1, k2, k3, k4 = jax.random.split(key, 4)
        inputs = jax.random.normal(k1, (B, N, DIN), dtype=jnp.float32)
        adj = (jax.random.uniform(k2, (B, N, N)) < EDGE_P).astype(jnp.float32)
        W = jax.random.normal(k3, (DIN, DOUT), dtype=jnp.float32) / np.sqrt(DIN)
        b = jax.random.normal(k4, (DOUT,), dtype=jnp.float32) * 0.01
        return {'inputs': inputs, 'adj': adj, 'W': W, 'b': b}
    _L1_gnn_all = _L1_gnn_setup()
    _L1_gnn_in = {k: v for k, v in _L1_gnn_all.items() if k in ('W', 'b')}
    del _L1_gnn_all
    return {'x': x, 'adj': adj, 'L0_gnn_W1': _L0_gnn_in['W1'], 'L0_gnn_b1': _L0_gnn_in['b1'], 'L0_gnn_gamma': _L0_gnn_in['gamma'], 'L0_gnn_beta': _L0_gnn_in['beta'], 'L0_gnn_W2': _L0_gnn_in['W2'], 'L0_gnn_b2': _L0_gnn_in['b2'], 'L1_gnn_W': _L1_gnn_in['W'], 'L1_gnn_b': _L1_gnn_in['b']}

def reference(x, adj, L0_gnn_W1, L0_gnn_b1, L0_gnn_gamma, L0_gnn_beta, L0_gnn_W2, L0_gnn_b2, L1_gnn_W, L1_gnn_b):
    import jax
    import jax.numpy as jnp

    def _L0_gnn_ref(x, adj, W1, b1, gamma, beta, W2, b2):
        import jax, jax.numpy as jnp
        import numpy as np
        EPS_LN = 1e-05

        def hypergraph_conv(x, adj, W, b):
            N, C, _ = adj.shape
            H = (adj != 0).astype(x.dtype)
            w = adj.reshape(N, -1)[:, :C]
            xw = jnp.einsum('ncd,hd->nch', x, W)
            Dn = jnp.einsum('nce,ne->nc', H, w)
            Dn = jnp.where(Dn > 0, 1.0 / Dn, 0.0)
            Be = H.sum(axis=1)
            Be = jnp.where(Be > 0, 1.0 / Be, 0.0)
            m = Be[:, :, None] * jnp.einsum('nce,nch->neh', H, xw)
            out = Dn[:, :, None] * jnp.einsum('nce,neh->nch', H, m)
            return out + b

        def layer_norm(x, g, b):
            mu = jnp.mean(x, axis=-1, keepdims=True)
            var = jnp.var(x, axis=-1, keepdims=True)
            return (x - mu) * jax.lax.rsqrt(var + EPS_LN) * g + b
        h = jax.nn.relu(hypergraph_conv(x, adj, W1, b1))
        h = layer_norm(h, gamma, beta)
        y = hypergraph_conv(h, adj, W2, b2)
        return y + x

    def _L1_gnn_ref(inputs, adj, W, b):
        import jax, jax.numpy as jnp
        import numpy as np
        B, N, DIN, DOUT = (8, 1024, 256, 256)
        EDGE_P = 0.01

        def _gcn_norm(adj):
            A = (adj != 0).astype(adj.dtype)
            eye = jnp.eye(A.shape[-1], dtype=A.dtype)
            A = jnp.maximum(A, eye)
            deg = A.sum(axis=-1)
            dinv = jnp.where(deg > 0, jax.lax.rsqrt(deg), 0.0)
            return dinv[..., :, None] * A * dinv[..., None, :]
        norm = _gcn_norm(adj)
        h = jnp.einsum('bnf,fo->bno', inputs, W)
        agg = jnp.einsum('bnm,bmo->bno', norm, h)
        return jnp.tanh(agg + b)
    x = _layernorm(x + _L0_gnn_ref(x, adj, L0_gnn_W1, L0_gnn_b1, L0_gnn_gamma, L0_gnn_beta, L0_gnn_W2, L0_gnn_b2), axis=-1)
    x = _layernorm(x + _L1_gnn_ref(x, adj, L1_gnn_W, L1_gnn_b), axis=-1)
    return x

_drawn_inputs = setup_inputs


def setup_inputs(seed=0):
    import zlib

    import numpy as np

    out = dict(_drawn_inputs(seed))
    spreads = {'L0_gnn_b1': (0.0, 0.1),
     'L0_gnn_gamma': (1.0, 0.2),
     'L0_gnn_beta': (0.0, 0.1),
     'L0_gnn_b2': (0.0, 0.1)}
    factors = {'L1_gnn_b': 7.775}
    for name, (base, spread) in spreads.items():
        noise = np.random.default_rng([zlib.crc32(name.encode()), seed]).standard_normal(out[name].shape)
        drawn = base * np.exp(spread * noise) if base else spread * noise
        out[name] = jnp.asarray(drawn.astype(out[name].dtype))
    for name, factor in factors.items():
        out[name] = (out[name] * factor).astype(out[name].dtype)
    return out
```

```python
import numpy as np
import concourse.bass as bass
from concourse import mybir
from contextlib import ExitStack

F32 = mybir.dt.float32
F32R = mybir.dt.float32r
BF16 = mybir.dt.bfloat16
ALU = mybir.AluOpType
ACT = mybir.ActivationFunctionType

EPS = 1e-5
TINY = 1.2e-38
AHEAD, BEHIND = 2, 3
UNROLL = 4


def bass_resnorm_graph_layers(nc, x, adj, W1, b1, gamma, beta, W2, b2, W, b, out):
    NG, C, D = x.shape
    DH = W1.shape[0]
    P = 128
    CT, DT, HT_ = C // P, D // P, DH // P
    assert CT == 2 and DT == 2 and HT_ == 4

    LOOP_FROM = UNROLL
    LOOP_TO = (NG - 4 - LOOP_FROM + 1) // UNROLL * UNROLL + LOOP_FROM
    FIRST, LAST = -AHEAD, NG - 1 + BEHIND

    def live(t, off):
        return not isinstance(t, int) or 0 <= t + off < NG

    def past(g, k):
        return not isinstance(g, int) or g >= k

    def run_slots(eng, slot):
        for t in range(FIRST, LOOP_FROM):
            slot(t, t % UNROLL)
        with eng.Fori(LOOP_FROM, LOOP_TO - UNROLL + 1, UNROLL) as t0:
            for k in range(UNROLL):
                slot(t0 + k, k)
        for t in range(LOOP_TO, LAST + 1):
            slot(t, t % UNROLL)

    def loaded(g, j):
        return (g - j) * 4 + 16

    ctx = ExitStack()
    with ctx:
        def sb(name, shape, dt=F32):
            return ctx.enter_context(nc.sbuf_tensor(name, shape, dt))

        def sem(name):
            return ctx.enter_context(nc.semaphore(name))

        ident_bf = sb("ident_bf", [P, P], BF16)
        ident = sb("ident", [P, P])
        ones_row = sb("ones_row", [1, P])
        mean_w = sb("mean_w", [P, P])
        tiny = sb("tiny", [P, CT])
        eps = sb("eps", [P, CT])
        minus = sb("minus", [P, CT])
        half_pow = sb("half_pow", [P, 4])
        Wn = sb("Wn", [P, DT, D])
        gcol = sb("gcol", [P, HT_])
        bcol = sb("bcol", [P, HT_])
        rows = sb("rows", [1, DH + 2 * D])
        ones_sq = sb("ones_sq", [P, P])
        beta_sq = sb("beta_sq", [P, HT_, P])
        Gc = sb("Gc", [P, HT_, D])
        gmean = sb("gmean", [P, D])
        W1hi, W1lo = sb("W1hi", [P, DT, DH], F32R), sb("W1lo", [P, DT, DH], F32R)
        Ghi, Glo = sb("Ghi", [P, HT_, D], F32R), sb("Glo", [P, HT_, D], F32R)
        Whi, Wlo = sb("Whi", [P, DT, D], F32R), sb("Wlo", [P, DT, D], F32R)
        b1_b = sb("b1_b", [P, DH])
        b2_b = sb("b2_b", [P, CT, D])
        bL_b = sb("bL_b", [P, D])
        bW_b = sb("bW_b", [P, D])

        adj_t = sb("adj_t", [P, 4, CT, C])
        x_t = sb("x_t", [P, 4, CT, D])
        wd_t = sb("wd_t", [P, 4, 2, CT])
        Hb = sb("Hb", [P, 2, CT, C], BF16)
        HT = sb("HT", [P, 4, CT, C], F32R)
        cnt = sb("cnt", [P, 2, CT])
        cnt1 = sb("cnt1", [P, 2, CT])
        Be = sb("Be", [P, 2, CT])
        Behi = sb("Behi", [P, 2, CT], F32R)
        Belo = sb("Belo", [P, 2, CT])
        HBhi, HBlo = sb("HBhi", [P, 2, CT, C + 2], F32R), sb("HBlo", [P, 2, CT, C + 2], F32R)
        xhi, xlo = sb("xhi", [P, 2, CT, D], F32R), sb("xlo", [P, 2, CT, D], F32R)
        Shi, Slo = sb("Shi", [P, 4, CT, C], F32R), sb("Slo", [P, 4, CT, C], F32R)
        sc_in = sb("sc_in", [P, 2, 4])
        sc_mask = sb("sc_mask", [P, 2, CT])
        sc = sb("sc", [P, 4, 4])
        Dn = sb("Dn", [P, 4, CT])
        uhi, ulo = sb("uhi", [P, 2, DT, C], F32R), sb("ulo", [P, 2, DT, C], F32R)
        z = sb("z", [P, 2, CT, DH])
        v = sb("v", [P, 2, CT, DH])
        W1n = z[:, 0].rearrange("p t (u d) -> p (t u) d", d=D)
        W2n = z[:, 1]
        W2T = v[:, 0].rearrange("p t (u d) -> p (t u) d", d=D)
        G = v[:, 1].rearrange("p t (u d) -> p (t u) d", d=D)
        bn_v, ag_v, rs_v = sb("bn_v", [P, CT, 6]), sb("ag_v", [P, 2, CT, 2]), sb("rs_v", [P, 2, CT])
        ve_v = sb("ve_v", [P, 2, CT])
        vhi, vlo = sb("vhi", [P, 2, HT_, C], F32R), sb("vlo", [P, 2, HT_, C], F32R)
        hw = sb("hw", [P, 2, CT, D])
        hwhi, hwlo = sb("hwhi", [P, 2, CT, D], F32R), sb("hwlo", [P, 2, CT, D], F32R)
        xb = sb("xb", [P, 2, CT, D])
        y = sb("y", [P, 2, CT, D])
        bn_y, ag_y, rs_y = sb("bn_y", [P, CT, 6]), sb("ag_y", [P, 2, CT, 2]), sb("rs_y", [P, 2, CT])
        ve_y, nm_y, nb_y = (sb(f"{n}_y", [P, 2, CT]) for n in ("ve", "nm", "nb"))
        x1 = sb("x1", [P, 4, CT, D])
        xdhi, xdlo = sb("xdhi", [P, 2, CT, D], F32R), sb("xdlo", [P, 2, CT, D], F32R)
        zhi, zlo = sb("zhi", [P, 2, DT, C], F32R), sb("zlo", [P, 2, DT, C], F32R)
        a_pre = sb("a_pre", [P, 2, CT, D])
        th = sb("th", [P, 2, CT, D])
        res = sb("res", [P, 2, CT, D])
        bn_o, ag_o, rs_o = sb("bn_o", [P, CT, 6]), sb("ag_o", [P, 2, CT, 2]), sb("rs_o", [P, 2, CT])
        ve_o, nm_o, nb_o = (sb(f"{n}_o", [P, 2, CT]) for n in ("ve", "nm", "nb"))
        out_t = sb("out_t", [P, 2, CT, D])

        ps = ctx.enter_context(nc.psum_tensor("ps", [P, 8, 512], F32))
        R_BANK, V_BANK = (0, 1), (0, 1)
        S_BANK, U_BANK, Z_BANK = (2, 3), 2, 3
        Y_BANK, A_BANK, W_BANK, HT_BANK = 4, 5, 6, 7
        psHT = ps[:, HT_BANK, 0:C].bitcast(BF16)

        s_w = sem("weights_in")
        s_adj = [sem(f"adj_in{j}") for j in range(4)]
        s_x = [sem(f"x_in{j}") for j in range(4)]
        s_wd = [sem(f"wd_in{j}") for j in range(4)]
        s_out = [sem(f"out_stored{j}") for j in range(2)]
        s_id0, s_id = sem("ident_zeroed"), sem("consts_made")
        s_cdve = sem("dve_consts_made")
        s_wps, s_wsb, s_gps, s_gsb, s_wend = (sem("weights_transposed"), sem("weights_copied"), sem("gamma_sums"),
                                              sem("mean_copied"), sem("weights_split"))
        p_ht, p_s, p_u = sem("ht_in_psum"), sem("s_in_psum"), sem("u_in_psum")
        p_r, p_v = sem("r_in_psum"), sem("vt_in_psum")
        p_w, p_y, p_z, p_a = sem("hw_in_psum"), sem("y_in_psum"), sem("z_in_psum"), sem("agg_in_psum")
        a_ht, a_hb, a_s, a_u = sem("ht_ready"), sem("hb_hi"), sem("s_hi"), sem("u_hi")
        a_relu, a_v = sem("relu_done"), sem("v_hi")
        a_w, a_xd, a_z, a_th, a_x = sem("hw_hi"), sem("xd_hi"), sem("z_hi"), sem("tanh_done"), sem("x_hi")
        a_x1, a_o = sem("x1_ready"), sem("out_ready")
        v_h, v_sc, v_s, v_at, v_u = (sem("h_ready"), sem("scalars_read"), sem("s_lo"),
                                           sem("at_ready"), sem("u_lo"))
        v_zb, v_v = sem("z_biased"), sem("v_lo")
        v_bnv, v_agv, v_bny, v_agy, v_bno, v_ago = (sem("v_bn"), sem("v_stats"), sem("y_bn"), sem("y_stats"),
                                                    sem("o_bn"), sem("o_stats"))
        v_w, v_y, v_xd, v_z, v_a, v_xb = (sem("hw_biased"), sem("y_summed"), sem("xd_lo"),
                                                     sem("z_lo"), sem("agg_biased"), sem("xb_ready"))
        g_ev, g_ey, g_eo = sem("v_var_eps"), sem("y_var_eps"), sem("o_var_eps")
        g_cnt = sem("cnt_guarded")
        g_be0, g_be1, g_be = sem("be_inverse"), sem("be_hi"), sem("be_ready")
        g_wc0, g_hb = sem("w_hi"), sem("hb_lo")
        g_sc, g_dn, g_x = sem("scalars_powered"), sem("dn_ready"), sem("x_lo")
        g_rv, g_w, g_ry, g_res, g_ro = sem("v_rstd"), sem("hw_lo"), sem("y_rstd"), sem("residual"), sem("o_rstd")

        block = ctx.enter_context(nc.Block())

        @block.sync
        def _(sp):
            def load_adj(g, j):
                sp.dma_start(adj_t[:, j], adj[g].rearrange("(t p) c -> p t c", p=P)).then_inc(s_adj[j], 16)

            def load_x(g, j):
                sp.dma_start(wd_t[:, j, 0], adj[g, 0].rearrange("(t p) -> p t", p=P), allow_slow_non_contiguous=True).then_inc(s_wd[j], 16)
                sp.dma_start(wd_t[:, j, 1], diag_of(g), allow_slow_non_contiguous=True).then_inc(s_wd[j], 16)
                sp.dma_start(x_t[:, j], x[g].rearrange("(t p) c -> p t c", p=P)).then_inc(s_x[j], 16)

            def diag_of(g):
                flat = adj[g].rearrange("a b -> (a b)")
                return bass.AP(tensor=flat.tensor, offset=flat.offset, ap=[[C + 1, P], [(C + 1) * P, CT]])

            load_adj(0, 0)
            sp.dma_start(W1n, W1.rearrange("(t p) d -> p t d", p=P)).then_inc(s_w, 16)
            sp.dma_start(W2n, W2.rearrange("(t p) d -> p t d", p=P)).then_inc(s_w, 16)
            sp.dma_start(gcol[:], gamma.rearrange("(t p) -> p t", p=P), allow_slow_non_contiguous=True).then_inc(s_w, 16)
            sp.dma_start(bcol[:], beta.rearrange("(t p) -> p t", p=P), allow_slow_non_contiguous=True).then_inc(s_w, 16)
            sp.dma_start(rows[0:1, 0:DH], b1.rearrange("(a n) -> a n", a=1)).then_inc(s_w, 16)
            sp.dma_start(rows[0:1, DH:DH + D], b2.rearrange("(a n) -> a n", a=1)).then_inc(s_w, 16)
            sp.dma_start(rows[0:1, DH + D:DH + 2 * D], b.rearrange("(a n) -> a n", a=1)).then_inc(s_w, 16)
            sp.dma_start(Wn[:], W.rearrange("(t p) d -> p t d", p=P)).then_inc(s_w, 16)
            load_x(0, 0)
            load_adj(1, 1)

            def slot(t, k):
                if live(t, 4):
                    if past(t, 0):
                        sp.wait_ge(v_h, t + 1)
                    load_adj(t + 4, k)
                if live(t, 3):
                    if past(t, 1):
                        sp.wait_ge(v_xb, t)
                        sp.wait_ge(v_sc, t)
                    load_x(t + 3, (k + 3) % 4)
                if live(t, -3):
                    sp.wait_ge(a_o, t - 2)
                    sp.dma_start(out[t - 3].rearrange("(t p) c -> p t c", p=P),
                                 out_t[:, (k + 1) % 2]).then_inc(s_out[(k + 1) % 2], 16)

            run_slots(sp, slot)
            for j in range(2):
                sp.wait_ge(s_out[j], 16 * NG // 2)

        @block.gpsimd
        def _(pool):
            nc.gpsimd.memset(ident[:], 0.0).then_inc(s_id0, 1)
            nc.gpsimd.memset(ones_row[:], 1.0).then_inc(s_id, 1)
            nc.gpsimd.memset(mean_w[:], 1.0 / DH).then_inc(s_id, 1)
            nc.gpsimd.memset(half_pow[:, 0:2], -1.0).then_inc(s_id, 1)
            nc.gpsimd.memset(half_pow[:, 2:4], -0.5).then_inc(s_id, 1)
            nc.gpsimd.memset(ones_sq[:], 1.0).then_inc(s_id, 1)
            nc.gpsimd.memset(tiny[:], TINY).then_inc(s_id, 1)
            nc.gpsimd.memset(eps[:], EPS).then_inc(s_id, 1)
            nc.gpsimd.memset(minus[:], -1.0).then_inc(s_id, 1)
            nc.gpsimd.memset(HBhi[:, :, :, C + 1:C + 2].bitcast(F32), 1.0).then_inc(s_id, 1)
            nc.gpsimd.memset(HBlo[:, :, :, C + 1:C + 2].bitcast(F32), 0.0).then_inc(s_id, 1)
            pool.wait_ge(s_id0, 1)
            nc.gpsimd.affine_select(out=ident[:], in_=ident[:], compare_op=ALU.not_equal, fill=1.0, base=0,
                                    pattern=[[-1, P]], channel_multiplier=1).then_inc(s_id, 1)
            pool.wait_ge(s_id, 11)
            nc.gpsimd.tensor_copy(ident_bf[:], ident[:]).then_inc(s_id, 1)

            def slot(t, k):
                if live(t, -1):
                    g, j2 = t - 1, (k + 1) % 2
                    pool.wait_ge(a_w, g + 1)
                    if past(g, 2):
                        pool.wait_ge(p_y, g - 1)
                    nc.gpsimd.tensor_tensor(hwlo[:, j2], hw[:, j2], hwhi[:, j2].bitcast(F32),
                                            ALU.subtract).then_inc(g_w, 1)
                if live(t, -3):
                    g, j2 = t - 3, (k + 1) % 2
                    pool.wait_ge(v_ago, g + 1)
                    nc.gpsimd.tensor_tensor(ve_o[:, j2], ag_o[:, j2, :, 1], eps[:], ALU.add).then_inc(g_eo, 1)
                    nc.gpsimd.tensor_tensor(nm_o[:, j2], ag_o[:, j2, :, 0], minus[:], ALU.mult).then_inc(g_eo, 1)
                    pool.wait_ge(g_eo, 2 * g + 2)
                    nc.gpsimd.tensor_tensor(rs_o[:, j2], ve_o[:, j2], half_pow[:, 2:4], ALU.pow).then_inc(g_ro, 1)
                    pool.wait_ge(g_ro, 2 * g + 1)
                    nc.gpsimd.tensor_tensor(nb_o[:, j2], nm_o[:, j2], rs_o[:, j2], ALU.mult).then_inc(g_ro, 1)
                if live(t, 1):
                    g, j, j2 = t + 1, (k + 1) % 4, (k + 1) % 2
                    pool.wait_ge(a_x, g + 1)
                    if past(g, 2):
                        pool.wait_ge(p_u, g - 1)
                    nc.gpsimd.tensor_tensor(xlo[:, j2], x_t[:, j], xhi[:, j2].bitcast(F32),
                                            ALU.subtract).then_inc(g_x, 1)
                if live(t, 2):
                    g, j, j2 = t + 2, (k + 2) % 4, k % 2
                    pool.wait_ge(s_wd[j], loaded(g, j) * 2)
                    if past(g, 2):
                        pool.wait_ge(p_s, g - 1)
                    nc.gpsimd.tensor_tensor(HBhi[:, j2, :, C], wd_t[:, j, 0], ones_sq[:, 0:CT],
                                            ALU.mult).then_inc(g_wc0, 1)
                if live(t, -1):
                    g, j2 = t - 1, (k + 1) % 2
                    pool.wait_ge(v_agy, g + 1)
                    nc.gpsimd.tensor_tensor(ve_y[:, j2], ag_y[:, j2, :, 1], eps[:], ALU.add).then_inc(g_ey, 1)
                    nc.gpsimd.tensor_tensor(nm_y[:, j2], ag_y[:, j2, :, 0], minus[:], ALU.mult).then_inc(g_ey, 1)
                    pool.wait_ge(g_ey, 2 * g + 2)
                    nc.gpsimd.tensor_tensor(rs_y[:, j2], ve_y[:, j2], half_pow[:, 2:4], ALU.pow).then_inc(g_ry, 1)
                    pool.wait_ge(g_ry, 2 * g + 1)
                    nc.gpsimd.tensor_tensor(nb_y[:, j2], nm_y[:, j2], rs_y[:, j2], ALU.mult).then_inc(g_ry, 1)
                if live(t, 0):
                    j2 = k % 2
                    pool.wait_ge(v_agv, t + 1)
                    nc.gpsimd.tensor_tensor(ve_v[:, j2], ag_v[:, j2, :, 1], eps[:], ALU.add).then_inc(g_ev, 1)
                    pool.wait_ge(g_ev, t + 1)
                    nc.gpsimd.tensor_tensor(rs_v[:, j2], ve_v[:, j2], half_pow[:, 2:4], ALU.pow).then_inc(g_rv, 1)
                if live(t, 2):
                    g, j, j2 = t + 2, (k + 2) % 4, k % 2
                    pool.wait_ge(a_ht, g + 1)
                    nc.gpsimd.tensor_tensor(cnt1[:, j2], cnt[:, j2], tiny[:], ALU.add).then_inc(g_cnt, 1)
                    pool.wait_ge(g_cnt, g + 1)
                    nc.gpsimd.tensor_tensor(Be[:, j2], cnt1[:, j2], half_pow[:, 0:CT], ALU.pow).then_inc(g_be0, 1)
                    pool.wait_ge(g_be0, g + 1)
                    nc.gpsimd.tensor_tensor(Behi[:, j2], Be[:, j2], ones_sq[:, 0:CT], ALU.mult).then_inc(g_be1, 1)
                    pool.wait_ge(g_wc0, g + 1)
                    nc.gpsimd.tensor_tensor(HBlo[:, j2, :, C], wd_t[:, j, 0], HBhi[:, j2, :, C].bitcast(F32),
                                            ALU.subtract)
                    pool.wait_ge(g_be1, g + 1)
                    nc.gpsimd.tensor_tensor(Belo[:, j2], Be[:, j2], Behi[:, j2].bitcast(F32),
                                            ALU.subtract).then_inc(g_be, 1)
                if live(t, 1):
                    g, j, j2 = t + 1, (k + 1) % 4, (k + 1) % 2
                    pool.wait_ge(v_sc, g + 1)
                    nc.gpsimd.tensor_tensor(sc[:, j], sc_in[:, j2], half_pow[:], ALU.pow).then_inc(g_sc, 1)
                if live(t, 2):
                    g, j, j2 = t + 2, (k + 2) % 4, k % 2
                    pool.wait_ge(g_be, g + 1)
                    nc.gpsimd.tensor_tensor(HBlo[:, j2, :, 0:C], HT[:, j].bitcast(F32),
                                            Belo[:, j2].unsqueeze(2).to_broadcast([P, CT, C]),
                                            ALU.mult).then_inc(g_hb, 1)
                if live(t, 1):
                    g, j, j2 = t + 1, (k + 1) % 4, (k + 1) % 2
                    pool.wait_ge(g_sc, g + 1)
                    nc.gpsimd.tensor_tensor(Dn[:, j], sc[:, j, 0:2], sc_mask[:, j2], ALU.mult).then_inc(g_dn, 1)
                if live(t, -2):
                    g, j, j2 = t - 2, (k + 2) % 4, k % 2
                    pool.wait_ge(a_th, g + 1)
                    nc.gpsimd.tensor_tensor(res[:, j2], x1[:, j], th[:, j2], ALU.add).then_inc(g_res, 1)

            run_slots(pool, slot)

        @block.scalar
        def _(act):
            def slot(t, k):
                if live(t, -1):
                    g, j2 = t - 1, (k + 1) % 2
                    act.wait_ge(v_w, g + 1)
                    if past(g, 2):
                        act.wait_ge(p_y, g - 1)
                    nc.scalar.copy(hwhi[:, j2], hw[:, j2]).then_inc(a_w, 1)
                if live(t, -2):
                    g, j2 = t - 2, k % 2
                    act.wait_ge(p_z, g + 1)
                    if past(g, 2):
                        act.wait_ge(p_a, g - 1)
                    nc.scalar.copy(zhi[:, j2].rearrange("p t c -> p (t c)"), ps[:, Z_BANK]).then_inc(a_z, 1)
                for c in range(CT):
                    if live(t, 0):
                        act.wait_ge(v_zb, 2 * t + c + 1)
                        if c == 0 and past(t, 2):
                            act.wait_ge(p_v, 2 * t - 2)
                        nc.scalar.activation(v[:, k % 2, c], z[:, k % 2, c], ACT.Relu).then_inc(a_relu, 1)
                    if c == 0 and live(t, 1):
                        g, j, j2 = t + 1, (k + 1) % 4, (k + 1) % 2
                        act.wait_ge(s_x[j], loaded(g, j))
                        if past(g, 2):
                            act.wait_ge(p_u, g - 1)
                        nc.scalar.copy(xhi[:, j2], x_t[:, j]).then_inc(a_x, 1)
                if live(t, 1):
                    g, j = t + 1, (k + 1) % 4
                    act.wait_ge(p_s, g + 1)
                    nc.scalar.copy(Shi[:, j], ps[:, S_BANK[0]:S_BANK[0] + 2, 0:C]).then_inc(a_s, 1)
                if live(t, 0):
                    j2 = k % 2
                    for q in range(2):
                        act.wait_ge(p_v, 2 * t + q + 1)
                        if q == 0 and past(t, 2):
                            act.wait_ge(p_w, t - 1)
                        nc.scalar.copy(vhi[:, j2, 2 * q:2 * q + 2].rearrange("p t c -> p (t c)"),
                                       ps[:, V_BANK[q]]).then_inc(a_v, 1)
                if live(t, 2):
                    g, j, j2 = t + 2, (k + 2) % 4, k % 2
                    act.wait_ge(p_ht, g + 1)
                    for e in range(CT):
                        last = nc.scalar.activation(HT[:, j, e], psHT[:, e * C:(e + 1) * C], ACT.Copy,
                                                    accum_out=cnt[:, j2, e:e + 1])
                    last.then_inc(a_ht, 1)
                if live(t, -1):
                    g, j, j2 = t - 1, (k + 3) % 4, (k + 1) % 2
                    act.wait_ge(g_ry, 2 * g + 2)
                    for c in range(CT):
                        last = nc.scalar.activation(x1[:, j, c], y[:, j2, c], ACT.Identity, bias=nb_y[:, j2, c:c + 1],
                                                    scale=rs_y[:, j2, c:c + 1])
                    last.then_inc(a_x1, 1)
                    act.wait_ge(a_x1, g + 1)
                    for c in range(CT):
                        last = nc.scalar.activation(xdhi[:, j2, c], x1[:, j, c], ACT.Copy, scale=sc[:, j, 2 + c:3 + c])
                    last.then_inc(a_xd, 1)
                if live(t, 1):
                    g, j2 = t + 1, (k + 1) % 2
                    act.wait_ge(p_u, g + 1)
                    nc.scalar.copy(uhi[:, j2].rearrange("p t c -> p (t c)"), ps[:, U_BANK]).then_inc(a_u, 1)
                if live(t, -2):
                    g, j2 = t - 2, k % 2
                    act.wait_ge(v_a, g + 1)
                    if past(g, 2):
                        act.wait_ge(g_res, g - 1)
                    nc.scalar.activation(th[:, j2], a_pre[:, j2], ACT.Tanh).then_inc(a_th, 1)
                if live(t, 2):
                    g, j, j2 = t + 2, (k + 2) % 4, k % 2
                    act.wait_ge(g_be1, g + 1)
                    for e in range(CT):
                        last = nc.scalar.activation(HBhi[:, j2, e, 0:C], HT[:, j, e].bitcast(F32), ACT.Copy,
                                                    scale=Behi[:, j2, e:e + 1].bitcast(F32))
                    last.then_inc(a_hb, 1)
                if live(t, -3):
                    g, j2 = t - 3, (k + 1) % 2
                    act.wait_ge(g_ro, 2 * g + 2)
                    if past(g, 2):
                        act.wait_ge(s_out[j2], (g - j2) * 8)
                    for c in range(CT):
                        last = nc.scalar.activation(out_t[:, j2, c], res[:, j2, c], ACT.Identity,
                                                    bias=nb_o[:, j2, c:c + 1], scale=rs_o[:, j2, c:c + 1])
                    last.then_inc(a_o, 1)

            run_slots(act, slot)

        @block.vector
        def _(dve):
            dve.wait_ge(s_w, 8 * 16)
            dve.wait_ge(s_id, 12)
            for h in range(HT_):
                last = nc.vector.tensor_scalar(beta_sq[:, h], ones_sq[:], bcol[:, h:h + 1], None, ALU.mult)
            last.then_inc(s_cdve, 1)
            nc.vector.tensor_copy(Whi[:], Wn[:]).then_inc(s_wend, 1)
            dve.wait_ge(s_wps, 1)
            nc.vector.tensor_copy(W1hi[:], ps[:, 0:2, 0:DH]).then_inc(s_wend, 1)
            for q in range(2):
                nc.vector.tensor_copy(W2T[:, 2 * q:2 * q + 2].rearrange("p t c -> p (t c)"),
                                      ps[:, 2 + q]).then_inc(s_wsb, 1)
            for q in range(2):
                for h in range(2):
                    last = nc.vector.tensor_scalar(G[:, 2 * q + h], ps[:, 2 + q, h * D:(h + 1) * D],
                                                   gcol[:, 2 * q + h:2 * q + h + 1], None, ALU.mult)
            last.then_inc(s_wsb, 1)
            dve.wait_ge(s_wend, 2)
            nc.vector.tensor_tensor(Wlo[:], Wn[:], Whi[:].bitcast(F32), ALU.subtract).then_inc(s_wend, 1)
            nc.vector.tensor_tensor(W1lo[:], ps[:, 0:2, 0:DH], W1hi[:].bitcast(F32), ALU.subtract).then_inc(s_wend, 1)
            dve.wait_ge(s_gps, 1)
            nc.vector.tensor_copy(bW_b[:], ps[:, 4, 0:D])
            nc.vector.tensor_copy(b1_b[:], ps[:, 6, 0:DH])
            for c in range(CT):
                nc.vector.tensor_copy(b2_b[:, c], ps[:, 7, 0:D])
            nc.vector.tensor_copy(bL_b[:], ps[:, 7, D:2 * D])
            nc.vector.tensor_copy(gmean[:], ps[:, 5, 0:D]).then_inc(s_gsb, 1)
            dve.wait_ge(s_gsb, 1)
            for h in range(HT_):
                last = nc.vector.tensor_tensor(Gc[:, h], G[:, h], gmean[:], ALU.subtract)
            last.then_inc(s_gsb, 1)
            dve.wait_ge(s_gsb, 2)
            nc.vector.tensor_copy(Ghi[:], Gc[:]).then_inc(s_gsb, 1)
            dve.wait_ge(s_gsb, 3)
            nc.vector.tensor_tensor(Glo[:], Gc[:], Ghi[:].bitcast(F32), ALU.subtract).then_inc(s_wend, 1)

            def slot(t, k):
                if live(t, -2):
                    g, j2 = t - 2, k % 2
                    dve.wait_ge(a_z, g + 1)
                    nc.vector.tensor_tensor(zlo[:, j2].rearrange("p t c -> p (t c)"), ps[:, Z_BANK],
                                            zhi[:, j2].rearrange("p t c -> p (t c)").bitcast(F32),
                                            ALU.subtract).then_inc(v_z, 1)
                if live(t, -3):
                    g, j2 = t - 3, (k + 1) % 2
                    dve.wait_ge(g_res, g + 1)
                    for c in range(CT):
                        last = nc.vector.bn_stats(bn_o[:, c], res[:, j2, c])
                    last.then_inc(v_bno, 1)
                for c in range(CT):
                    if live(t, 0):
                        if c == 0:
                            dve.wait_ge(g_dn, t + 1)
                        dve.wait_ge(p_r, 2 * t + c + 1)
                        nc.vector.scalar_tensor_tensor(z[:, k % 2, c], ps[:, R_BANK[c], 0:DH], Dn[:, k, c:c + 1],
                                                       b1_b[:], ALU.mult, ALU.add).then_inc(v_zb, 1)
                    if c == 0 and live(t, 0):
                        nc.vector.scalar_tensor_tensor(xb[:, k % 2], x_t[:, k], 2.0, b2_b[:],
                                                       ALU.mult, ALU.add).then_inc(v_xb, 1)
                if live(t, 2):
                    g, j, j2 = t + 2, (k + 2) % 4, k % 2
                    dve.wait_ge(s_adj[j], loaded(g, j))
                    if past(g, 2):
                        dve.wait_ge(p_ht, g - 1)
                    if live(t, -3):
                        dve.wait_ge(v_bno, t - 2)
                    nc.vector.tensor_scalar(Hb[:, j2], adj_t[:, j], 0.0, None, ALU.not_equal).then_inc(v_h, 1)
                if live(t, -3):
                    if not live(t, 2):
                        dve.wait_ge(v_bno, t - 2)
                    for c in range(CT):
                        last = nc.vector.bn_aggr(ag_o[:, (k + 1) % 2, c], bn_o[:, c])
                    last.then_inc(v_ago, 1)
                if live(t, 0):
                    dve.wait_ge(a_relu, 2 * t + 1)
                    nc.vector.bn_stats(bn_v[:, 0], v[:, k % 2, 0])
                if live(t, -1):
                    g, j, j2 = t - 1, (k + 3) % 4, (k + 1) % 2
                    dve.wait_ge(p_y, g + 1)
                    dve.wait_ge(v_xb, g + 1)
                    for c in range(CT):
                        last = nc.vector.scalar_tensor_tensor(y[:, j2, c], ps[:, Y_BANK, c * D:(c + 1) * D],
                                                              Dn[:, j, c:c + 1], xb[:, j2, c], ALU.mult, ALU.add)
                    last.then_inc(v_y, 1)
                if live(t, 0):
                    dve.wait_ge(a_relu, 2 * t + 2)
                    nc.vector.bn_stats(bn_v[:, 1], v[:, k % 2, 1]).then_inc(v_bnv, 1)
                if live(t, -1):
                    g, j2 = t - 1, (k + 1) % 2
                    dve.wait_ge(v_y, g + 1)
                    for c in range(CT):
                        last = nc.vector.bn_stats(bn_y[:, c], y[:, j2, c])
                    last.then_inc(v_bny, 1)
                if live(t, 1):
                    g, j, j2 = t + 1, (k + 1) % 4, (k + 1) % 2
                    dve.wait_ge(a_s, g + 1)
                    if past(g, 2):
                        dve.wait_ge(g_dn, g - 1)
                    if live(t, 0):
                        dve.wait_ge(v_bnv, t + 1)
                    if live(t, -1):
                        dve.wait_ge(v_bny, t)
                    d_col = ps[:, S_BANK[0]:S_BANK[0] + 2, C]
                    rc_col = ps[:, S_BANK[0]:S_BANK[0] + 2, C + 1]
                    nc.vector.tensor_scalar(sc_in[:, j2, 0:2], d_col, TINY, None, ALU.max)
                    nc.vector.tensor_scalar(sc_mask[:, j2], d_col, 0.0, None, ALU.is_gt)
                    nc.vector.scalar_tensor_tensor(sc_in[:, j2, 2:4], wd_t[:, j, 1], 0.0, rc_col,
                                                   ALU.is_equal, ALU.add).then_inc(v_sc, 1)
                if live(t, -1):
                    if not live(t, 1):
                        dve.wait_ge(v_bny, t)
                    for c in range(CT):
                        last = nc.vector.bn_aggr(ag_y[:, (k + 1) % 2, c], bn_y[:, c])
                    last.then_inc(v_agy, 1)
                if live(t, 1):
                    g, j = t + 1, (k + 1) % 4
                    nc.vector.tensor_tensor(Slo[:, j], ps[:, S_BANK[0]:S_BANK[0] + 2, 0:C], Shi[:, j].bitcast(F32),
                                            ALU.subtract).then_inc(v_s, 1)
                if live(t, 0):
                    j2 = k % 2
                    for q in range(2):
                        dve.wait_ge(a_v, 2 * t + q + 1)
                        nc.vector.tensor_tensor(vlo[:, j2, 2 * q:2 * q + 2].rearrange("p t c -> p (t c)"),
                                                ps[:, V_BANK[q]],
                                                vhi[:, j2, 2 * q:2 * q + 2].rearrange("p t c -> p (t c)").bitcast(F32),
                                                ALU.subtract).then_inc(v_v, 1)
                if live(t, 0):
                    if not live(t, 1):
                        dve.wait_ge(v_bnv, t + 1)
                    for c in range(CT):
                        last = nc.vector.bn_aggr(ag_v[:, k % 2, c], bn_v[:, c])
                    last.then_inc(v_agv, 1)
                if live(t, -2):
                    g, j, j2 = t - 2, (k + 2) % 4, k % 2
                    dve.wait_ge(p_a, g + 1)
                    for c in range(CT):
                        last = nc.vector.scalar_tensor_tensor(a_pre[:, j2, c], ps[:, A_BANK, c * D:(c + 1) * D],
                                                              sc[:, j, 2 + c:3 + c], bL_b[:], ALU.mult, ALU.add)
                    last.then_inc(v_a, 1)
                if live(t, 1):
                    j = (k + 1) % 4
                    for c in range(CT):
                        blk = HT[:, j, c, c * P:(c + 1) * P]
                        last = nc.vector.tensor_tensor(blk, blk.bitcast(F32), ident[:], ALU.max)
                    last.then_inc(v_at, 1)
                if live(t, 1):
                    g, j2 = t + 1, (k + 1) % 2
                    dve.wait_ge(a_u, g + 1)
                    nc.vector.tensor_tensor(ulo[:, j2].rearrange("p t c -> p (t c)"), ps[:, U_BANK],
                                            uhi[:, j2].rearrange("p t c -> p (t c)").bitcast(F32),
                                            ALU.subtract).then_inc(v_u, 1)
                if live(t, -1):
                    g, j, j2 = t - 1, (k + 3) % 4, (k + 1) % 2
                    dve.wait_ge(a_xd, g + 1)
                    for c in range(CT):
                        last = nc.vector.scalar_tensor_tensor(xdlo[:, j2, c], x1[:, j, c], sc[:, j, 2 + c:3 + c],
                                                              xdhi[:, j2, c].bitcast(F32), ALU.mult, ALU.subtract)
                    last.then_inc(v_xd, 1)
                if live(t, 0):
                    j2 = k % 2
                    dve.wait_ge(p_w, t + 1)
                    dve.wait_ge(g_rv, t + 1)
                    if past(t, 2):
                        dve.wait_ge(g_w, t - 1)
                    for c in range(CT):
                        last = nc.vector.scalar_tensor_tensor(hw[:, j2, c], ps[:, W_BANK, c * D:(c + 1) * D],
                                                              rs_v[:, j2, c:c + 1], bW_b[:], ALU.mult, ALU.add)
                    last.then_inc(v_w, 1)

            run_slots(dve, slot)

        @block.tensor
        def _(pe):
            def product(out_ap, pairs, kt):
                n, total = 0, len(pairs) * kt
                for left, right in pairs:
                    for q in range(kt):
                        last = nc.tensor.matmul(out_ap, left(q), right(q), start=(n == 0), stop=(n == total - 1))
                        n += 1
                return last

            def three(lhi, llo, rhi, rlo):
                return [(lhi, rhi), (lhi, rlo), (llo, rhi)]

            pe.wait_ge(s_w, 8 * 16)
            pe.wait_ge(s_id, 12)
            for d in range(DT):
                for h in range(HT_):
                    nc.tensor.transpose(ps[:, d, h * P:(h + 1) * P], W1n[:, h, d * P:(d + 1) * P], ident[:])
            for h in range(HT_):
                for o in range(DT):
                    q = (h % 2) * D + o * P
                    last = nc.tensor.transpose(ps[:, 2 + h // 2, q:q + P], W2n[:, o, h * P:(h + 1) * P], ident[:])
            last.then_inc(s_wps, 1)
            nc.tensor.matmul(ps[:, 6, 0:DH], ones_row[:], rows[0:1, 0:DH], start=True, stop=True)
            nc.tensor.matmul(ps[:, 7, 0:2 * D], ones_row[:], rows[0:1, DH:DH + 2 * D], start=True, stop=True)
            pe.wait_ge(s_cdve, 1)
            pe.wait_ge(s_wsb, 3)
            product(ps[:, 4, 0:D], [(lambda q: beta_sq[:, q], lambda q: W2T[:, q])], HT_)
            product(ps[:, 5, 0:D], [(lambda q: mean_w[:], lambda q: G[:, q])], HT_).then_inc(s_gps, 1)
            pe.wait_ge(s_wend, 5)

            def slot(t, k):
                if live(t, 0):
                    j2 = k % 2
                    pe.wait_ge(v_u, t + 1)
                    for c in range(CT):
                        if past(t, 1):
                            pe.wait_ge(v_v, 2 * t - 1 + c)
                        cs = slice(c * P, (c + 1) * P)
                        product(ps[:, R_BANK[c], 0:DH],
                                three(lambda q: uhi[:, j2, q, cs], lambda q: ulo[:, j2, q, cs],
                                      lambda q: W1hi[:, q], lambda q: W1lo[:, q]), DT).then_inc(p_r, 1)
                if live(t, -1):
                    g, j, j2 = t - 1, (k + 3) % 4, (k + 1) % 2
                    pe.wait_ge(g_w, g + 1)
                    if past(g, 1):
                        pe.wait_ge(v_y, g)
                    for c in range(CT):
                        cs = slice(c * P, (c + 1) * P)
                        last = product(ps[:, Y_BANK, c * D:(c + 1) * D],
                                       three(lambda q: Shi[:, j, q, cs], lambda q: Slo[:, j, q, cs],
                                             lambda q: hwhi[:, j2, q], lambda q: hwlo[:, j2, q]), CT)
                    last.then_inc(p_y, 1)
                if live(t, 1):
                    g, j, j2 = t + 1, (k + 1) % 4, (k + 1) % 2
                    pe.wait_ge(a_hb, g + 1)
                    pe.wait_ge(g_hb, g + 1)
                    if past(g, 1):
                        pe.wait_ge(v_u, g)
                    if past(g, 3):
                        pe.wait_ge(v_z, g - 2)
                    for c in range(CT):
                        cs = slice(c * P, (c + 1) * P)
                        last = product(ps[:, S_BANK[c], 0:C + 2],
                                       [(lambda q: HT[:, j, q, cs], lambda q: HBhi[:, j2, q]),
                                        (lambda q: HT[:, j, q, cs], lambda q: HBlo[:, j2, q])], CT)
                    last.then_inc(p_s, 1)
                if live(t, 0):
                    j2 = k % 2
                    pe.wait_ge(a_relu, 2 * t + 2)
                    for q in range(2):
                        for h in range(2):
                            for c in range(CT):
                                at = h * C + c * P
                                last = nc.tensor.transpose(ps[:, V_BANK[q], at:at + P],
                                                           v[:, j2, c, (2 * q + h) * P:(2 * q + h + 1) * P], ident[:])
                        last.then_inc(p_v, 1)
                if live(t, -2):
                    g, j2 = t - 2, k % 2
                    pe.wait_ge(v_z, g + 1)
                    if past(g, 1):
                        pe.wait_ge(v_a, g)
                    for c in range(CT):
                        cs = slice(c * P, (c + 1) * P)
                        last = product(ps[:, A_BANK, c * D:(c + 1) * D],
                                       three(lambda q: zhi[:, j2, q, cs], lambda q: zlo[:, j2, q, cs],
                                             lambda q: Whi[:, q], lambda q: Wlo[:, q]), DT)
                    last.then_inc(p_a, 1)
                if live(t, 2):
                    g, j2 = t + 2, k % 2
                    pe.wait_ge(v_h, g + 1)
                    if past(g, 1):
                        pe.wait_ge(a_ht, g)
                    for e in range(CT):
                        for c in range(CT):
                            last = nc.tensor.transpose(psHT[:, e * C + c * P:e * C + (c + 1) * P],
                                                       Hb[:, j2, c, e * P:(e + 1) * P], ident_bf[:])
                    last.then_inc(p_ht, 1)
                if live(t, 1):
                    g, j, j2 = t + 1, (k + 1) % 4, (k + 1) % 2
                    pe.wait_ge(g_x, g + 1)
                    pe.wait_ge(v_s, g + 1)
                    for d in range(DT):
                        cs = slice(d * P, (d + 1) * P)
                        last = product(ps[:, U_BANK, d * C:(d + 1) * C],
                                       three(lambda q: xhi[:, j2, q, cs], lambda q: xlo[:, j2, q, cs],
                                             lambda q: Shi[:, j, q], lambda q: Slo[:, j, q]), CT)
                    last.then_inc(p_u, 1)
                if live(t, 0):
                    j2 = k % 2
                    pe.wait_ge(v_v, 2 * t + 2)
                    if past(t, 1):
                        pe.wait_ge(v_w, t)
                    for c in range(CT):
                        cs = slice(c * P, (c + 1) * P)
                        last = product(ps[:, W_BANK, c * D:(c + 1) * D],
                                       three(lambda q: vhi[:, j2, q, cs], lambda q: vlo[:, j2, q, cs],
                                             lambda q: Ghi[:, q], lambda q: Glo[:, q]), HT_)
                    last.then_inc(p_w, 1)
                if live(t, -1):
                    g, j, j2 = t - 1, (k + 3) % 4, (k + 1) % 2
                    pe.wait_ge(v_xd, g + 1)
                    pe.wait_ge(v_at, g + 1)
                    if past(g, 1):
                        pe.wait_ge(v_z, g)
                    for d in range(DT):
                        cs = slice(d * P, (d + 1) * P)
                        last = product(ps[:, Z_BANK, d * C:(d + 1) * C],
                                       [(lambda q: xdhi[:, j2, q, cs], lambda q: HT[:, j, q]),
                                        (lambda q: xdlo[:, j2, q, cs], lambda q: HT[:, j, q])], CT)
                    last.then_inc(p_z, 1)
            run_slots(pe, slot)


_INS = ['x', 'adj', 'L0_gnn_W1', 'L0_gnn_b1', 'L0_gnn_gamma', 'L0_gnn_beta', 'L0_gnn_W2', 'L0_gnn_b2',
        'L1_gnn_W', 'L1_gnn_b']


def kernel(**inputs):
    import numpy as _np
    import concourse.bacc as _bacc
    from concourse import mybir as _mybir
    from concourse.bass_utils import run_bass_kernel_spmd as _run

    nc = _bacc.Bacc("TRN2", target_bir_lowering=False, num_devices=1)
    arrays, args = {}, []
    for name in _INS:
        a = _np.ascontiguousarray(inputs[name])
        arrays[f"in_{name}_dram"] = a
        args.append(nc.dram_tensor(f"in_{name}_dram", a.shape, _mybir.dt.from_np(a.dtype), kind="ExternalInput").ap())
    shape = arrays["in_x_dram"].shape
    out = nc.dram_tensor("out_0_dram", shape, _mybir.dt.from_np(_np.dtype("float32")), kind="ExternalOutput").ap()
    bass_resnorm_graph_layers(nc, *args, out)
    r = _run(nc, [arrays], core_ids=[0])
    return r.results[0]["out_0_dram"]
```

```python
import numpy as np
import concourse.bass as bass
from concourse import mybir
from contextlib import ExitStack

F32 = mybir.dt.float32
F32R = mybir.dt.float32r
BF16 = mybir.dt.bfloat16
ALU = mybir.AluOpType
ACT = mybir.ActivationFunctionType

EPS = 1e-5
TINY = 1.2e-38
AHEAD, BEHIND = 4, 4
PEELED = 6
UNROLL = 4


def bass_resnorm_graph_layers(nc, x, adj, W1, b1, gamma, beta, W2, b2, W, b, out):
    NG, C, D = x.shape
    DH = W1.shape[0]
    P = 128
    CT, DT, HT_ = C // P, D // P, DH // P
    assert CT == 2 and DT == 2 and HT_ == 4

    LOOP_FROM = PEELED
    LOOP_TO = (NG - AHEAD - LOOP_FROM) // UNROLL * UNROLL + LOOP_FROM
    FIRST, LAST = -AHEAD, NG - 1 + BEHIND

    def live(t, off):
        return not isinstance(t, int) or 0 <= t + off < NG

    def run_slots(eng, slot):
        for t in range(FIRST, LOOP_FROM):
            slot(t, t % UNROLL)
        with eng.Fori(LOOP_FROM, LOOP_TO - UNROLL + 1, UNROLL) as t0:
            for k in range(UNROLL):
                slot(t0 + k, (LOOP_FROM + k) % UNROLL)
        for t in range(LOOP_TO, LAST + 1):
            slot(t, t % UNROLL)

    def loaded(g, j):
        return (g - j) * 4 + 16

    ctx = ExitStack()
    with ctx:
        def sb(name, shape, dt=F32):
            return ctx.enter_context(nc.sbuf_tensor(name, shape, dt))

        def sem(name):
            return ctx.enter_context(nc.semaphore(name))

        ident_bf = sb("ident_bf", [P, P], BF16)
        ident = sb("ident", [P, P])
        ones_row = sb("ones_row", [1, P])
        mean_w = sb("mean_w", [P, P])
        tiny = sb("tiny", [P, CT])
        eps = sb("eps", [P, CT])
        minus = sb("minus", [P, CT])
        half_pow = sb("half_pow", [P, 4])
        Wn = sb("Wn", [P, DT, D])
        gcol = sb("gcol", [P, HT_])
        bcol = sb("bcol", [P, HT_])
        rows = sb("rows", [1, DH + 2 * D])
        ones_sq = sb("ones_sq", [P, P])
        beta_sq = sb("beta_sq", [P, HT_, P])
        Gc = sb("Gc", [P, HT_, D])
        gmean = sb("gmean", [P, D])
        W1hi, W1lo = sb("W1hi", [P, DT, DH], F32R), sb("W1lo", [P, DT, DH], F32R)
        Ghi, Glo = sb("Ghi", [P, HT_, D], F32R), sb("Glo", [P, HT_, D], F32R)
        Whi, Wlo = sb("Whi", [P, DT, D], F32R), sb("Wlo", [P, DT, D], F32R)
        b1_b = sb("b1_b", [P, DH])
        b2_b = sb("b2_b", [P, CT, D])
        bL_b = sb("bL_b", [P, D])
        bW_b = sb("bW_b", [P, D])

        adj_t = sb("adj_t", [P, 4, CT, C])
        x_t = sb("x_t", [P, 4, CT, D])
        wd_t = sb("wd_t", [P, 4, 2, CT])
        Hb = sb("Hb", [P, 2, CT, C], BF16)
        HT = sb("HT", [P, 4, CT, C], F32R)
        cnt = sb("cnt", [P, 2, CT])
        cnt1 = sb("cnt1", [P, 2, CT])
        Be = sb("Be", [P, 2, CT])
        Behi = sb("Behi", [P, 2, CT], F32R)
        Belo = sb("Belo", [P, 2, CT])
        HBhi, HBlo = sb("HBhi", [P, 2, CT, C + 2], F32R), sb("HBlo", [P, 2, CT, C + 2], F32R)
        xhi, xlo = sb("xhi", [P, 2, CT, D], F32R), sb("xlo", [P, 2, CT, D], F32R)
        Shi, Slo = sb("Shi", [P, 4, CT, C], F32R), sb("Slo", [P, 4, CT, C], F32R)
        sc_in = sb("sc_in", [P, 2, 4])
        sc_mask = sb("sc_mask", [P, 2, CT])
        sc = sb("sc", [P, 4, 4])
        Dn = sb("Dn", [P, 4, CT])
        uhi, ulo = sb("uhi", [P, 2, DT, C], F32R), sb("ulo", [P, 2, DT, C], F32R)
        z = sb("z", [P, 2, CT, DH])
        v = sb("v", [P, 2, CT, DH])
        W1n = z[:, 0].rearrange("p t (u d) -> p (t u) d", d=D)
        W2n = z[:, 1]
        W2T = v[:, 0].rearrange("p t (u d) -> p (t u) d", d=D)
        G = v[:, 1].rearrange("p t (u d) -> p (t u) d", d=D)
        bn_v, ag_v, rs_v = sb("bn_v", [P, CT, 6]), sb("ag_v", [P, 2, CT, 2]), sb("rs_v", [P, 2, CT])
        ve_v = sb("ve_v", [P, 2, CT])
        vhi, vlo = sb("vhi", [P, 2, HT_, C], F32R), sb("vlo", [P, 2, HT_, C], F32R)
        hw = sb("hw", [P, 2, CT, D])
        hwhi, hwlo = sb("hwhi", [P, 2, CT, D], F32R), sb("hwlo", [P, 2, CT, D], F32R)
        xb = sb("xb", [P, 2, CT, D])
        y = sb("y", [P, 2, CT, D])
        bn_y, ag_y, rs_y = sb("bn_y", [P, CT, 6]), sb("ag_y", [P, 2, CT, 2]), sb("rs_y", [P, 2, CT])
        ve_y, nm_y, nb_y = (sb(f"{n}_y", [P, 2, CT]) for n in ("ve", "nm", "nb"))
        x1 = sb("x1", [P, 4, CT, D])
        xdhi, xdlo = sb("xdhi", [P, 2, CT, D], F32R), sb("xdlo", [P, 2, CT, D], F32R)
        zhi, zlo = sb("zhi", [P, 2, DT, C], F32R), sb("zlo", [P, 2, DT, C], F32R)
        a_pre = sb("a_pre", [P, 2, CT, D])
        th = sb("th", [P, 2, CT, D])
        res = sb("res", [P, 2, CT, D])
        bn_o, ag_o, rs_o = sb("bn_o", [P, CT, 6]), sb("ag_o", [P, 2, CT, 2]), sb("rs_o", [P, 2, CT])
        ve_o, nm_o, nb_o = (sb(f"{n}_o", [P, 2, CT]) for n in ("ve", "nm", "nb"))
        out_t = sb("out_t", [P, 2, CT, D])

        ps = ctx.enter_context(nc.psum_tensor("ps", [P, 8, 512], F32))
        R_BANK, V_BANK = (0, 1), (0, 1)
        S_BANK, U_BANK, Z_BANK = (2, 3), 2, 3
        Y_BANK, A_BANK, W_BANK, HT_BANK = 4, 5, 6, 7
        psHT = ps[:, HT_BANK, 0:C].bitcast(BF16)

        s_w = sem("weights_in")
        s_adj = [sem(f"adj_in{j}") for j in range(4)]
        s_x = [sem(f"x_in{j}") for j in range(4)]
        s_wd = [sem(f"wd_in{j}") for j in range(4)]
        s_out = [sem(f"out_stored{j}") for j in range(2)]
        s_id0, s_id = sem("ident_zeroed"), sem("consts_made")
        s_cdve = sem("dve_consts_made")
        s_wps, s_wsb, s_gps, s_gsb, s_wend = (sem("weights_transposed"), sem("weights_copied"), sem("gamma_sums"),
                                              sem("mean_copied"), sem("weights_split"))
        p_ht, p_s, p_u, p_r0, p_r1 = (
            sem(n) for n in ("ht_in_psum", "s_in_psum", "u_in_psum", "r_in_psum0", "r_in_psum1"))
        p_v0, p_v1, p_w, p_y, p_z = (
            sem(n) for n in ("vt_in_psum0", "vt_in_psum1", "hw_in_psum", "y_in_psum", "z_in_psum"))
        p_a = sem("agg_in_psum")
        a_ht, a_hb, a_s, a_u, a_x = (
            sem(n) for n in ("ht_ready", "hb_hi", "s_hi", "u_hi", "x_hi"))
        a_relu0, a_relu1, a_v0, a_v1, a_w = (
            sem(n) for n in ("relu_done0", "relu_done1", "v_hi0", "v_hi1", "hw_hi"))
        a_xd, a_z, a_th, a_x1, a_o = (
            sem(n) for n in ("xd_hi", "z_hi", "tanh_done", "x1_ready", "out_ready"))
        v_h, v_sc, v_s, v_at, v_u = (
            sem(n) for n in ("h_ready", "scalars_read", "s_lo", "at_ready", "u_lo"))
        v_z0, v_z1, v_v0, v_v1, v_bnv0 = (
            sem(n) for n in ("z_biased0", "z_biased1", "v_lo0", "v_lo1", "v_bn0"))
        v_bnv1, v_agv, v_bny, v_agy, v_bno = (
            sem(n) for n in ("v_bn1", "v_stats", "y_bn", "y_stats", "o_bn"))
        v_ago, v_w, v_y, v_xd, v_z = (
            sem(n) for n in ("o_stats", "hw_biased", "y_summed", "xd_lo", "z_lo"))
        v_a, v_xb = (
            sem(n) for n in ("agg_biased", "xb_ready"))
        g_ev, g_ey, g_eo, g_cnt, g_be = (
            sem(n) for n in ("v_var_eps", "y_var_eps", "o_var_eps", "cnt_guarded", "be_inverse"))
        g_behi, g_belo, g_wc, g_hb, g_sc = (
            sem(n) for n in ("be_hi", "be_lo", "w_hi", "hb_lo", "scalars_powered"))
        g_dn, g_x, g_rv, g_w, g_ry = (
            sem(n) for n in ("dn_ready", "x_lo", "v_rstd", "hw_lo", "y_rstd"))
        g_nby, g_res, g_ro, g_nbo = (
            sem(n) for n in ("y_shift", "residual", "o_rstd", "o_shift"))

        block = ctx.enter_context(nc.Block())

        @block.sync
        def _(sp):
            def load_adj(g, j):
                sp.dma_start(adj_t[:, j], adj[g].rearrange("(t p) c -> p t c", p=P)).then_inc(s_adj[j], 16)

            def load_x(g, j):
                sp.dma_start(wd_t[:, j, 0], adj[g, 0].rearrange("(t p) -> p t", p=P), allow_slow_non_contiguous=True).then_inc(s_wd[j], 16)
                sp.dma_start(wd_t[:, j, 1], diag_of(g), allow_slow_non_contiguous=True).then_inc(s_wd[j], 16)
                sp.dma_start(x_t[:, j], x[g].rearrange("(t p) c -> p t c", p=P)).then_inc(s_x[j], 16)

            def diag_of(g):
                flat = adj[g].rearrange("a b -> (a b)")
                return bass.AP(tensor=flat.tensor, offset=flat.offset, ap=[[C + 1, P], [(C + 1) * P, CT]])

            sp.dma_start(W1n, W1.rearrange("(t p) d -> p t d", p=P)).then_inc(s_w, 16)
            sp.dma_start(W2n, W2.rearrange("(t p) d -> p t d", p=P)).then_inc(s_w, 16)
            sp.dma_start(gcol[:], gamma.rearrange("(t p) -> p t", p=P), allow_slow_non_contiguous=True).then_inc(s_w, 16)
            sp.dma_start(bcol[:], beta.rearrange("(t p) -> p t", p=P), allow_slow_non_contiguous=True).then_inc(s_w, 16)
            sp.dma_start(rows[0:1, 0:DH], b1.rearrange("(a n) -> a n", a=1)).then_inc(s_w, 16)
            sp.dma_start(rows[0:1, DH:DH + D], b2.rearrange("(a n) -> a n", a=1)).then_inc(s_w, 16)
            sp.dma_start(rows[0:1, DH + D:DH + 2 * D], b.rearrange("(a n) -> a n", a=1)).then_inc(s_w, 16)
            sp.dma_start(Wn[:], W.rearrange("(t p) d -> p t d", p=P)).then_inc(s_w, 16)

            def slot(t, k):
                if live(t, 4):
                    g, j = t + 4, (k + 0) % 4
                    if live(g, -4):
                        sp.wait_ge(v_h, g - 3)
                    load_adj(g, j)
                if live(t, 4):
                    g, j = t + 4, (k + 0) % 4
                    if live(g, -4):
                        sp.wait_ge(v_xb, g - 3)
                    load_x(g, j)
                if live(t, -4):
                    g, j2 = t - 4, k % 2
                    sp.wait_ge(a_o, g + 1)
                    sp.dma_start(out[g].rearrange("(t p) c -> p t c", p=P), out_t[:, j2]).then_inc(s_out[j2], 16)

            run_slots(sp, slot)
            for j in range(2):
                sp.wait_ge(s_out[j], 16 * NG // 2)

        @block.gpsimd
        def _(pool):
            nc.gpsimd.memset(ident[:], 0.0).then_inc(s_id0, 1)
            nc.gpsimd.memset(ones_row[:], 1.0).then_inc(s_id, 1)
            nc.gpsimd.memset(mean_w[:], 1.0 / DH).then_inc(s_id, 1)
            nc.gpsimd.memset(half_pow[:, 0:2], -1.0).then_inc(s_id, 1)
            nc.gpsimd.memset(half_pow[:, 2:4], -0.5).then_inc(s_id, 1)
            nc.gpsimd.memset(ones_sq[:], 1.0).then_inc(s_id, 1)
            nc.gpsimd.memset(tiny[:], TINY).then_inc(s_id, 1)
            nc.gpsimd.memset(eps[:], EPS).then_inc(s_id, 1)
            nc.gpsimd.memset(minus[:], -1.0).then_inc(s_id, 1)
            nc.gpsimd.memset(HBhi[:, :, :, C + 1:C + 2].bitcast(F32), 1.0).then_inc(s_id, 1)
            nc.gpsimd.memset(HBlo[:, :, :, C + 1:C + 2].bitcast(F32), 0.0).then_inc(s_id, 1)
            pool.wait_ge(s_id0, 1)
            nc.gpsimd.affine_select(out=ident[:], in_=ident[:], compare_op=ALU.not_equal, fill=1.0, base=0,
                                    pattern=[[-1, P]], channel_multiplier=1).then_inc(s_id, 1)
            pool.wait_ge(s_id, 11)
            nc.gpsimd.tensor_copy(ident_bf[:], ident[:]).then_inc(s_id, 1)

            def slot(t, k):
                if live(t, 1):
                    g, j, j2 = t + 1, (k + 1) % 4, (k + 1) % 2
                    pool.wait_ge(g_behi, g + 1)
                    nc.gpsimd.tensor_tensor(HBlo[:, j2, :, C], wd_t[:, j, 0], HBhi[:, j2, :, C].bitcast(F32), ALU.subtract)
                    nc.gpsimd.tensor_tensor(Belo[:, j2], Be[:, j2], Behi[:, j2].bitcast(F32), ALU.subtract).then_inc(g_belo, 1)
                if live(t, -1):
                    g, j2 = t - 1, (k + 1) % 2
                    pool.wait_ge(a_w, g + 1)
                    nc.gpsimd.tensor_tensor(hwlo[:, j2], hw[:, j2], hwhi[:, j2].bitcast(F32), ALU.subtract).then_inc(g_w, 1)
                if live(t, 1):
                    g, j, j2 = t + 1, (k + 1) % 4, (k + 1) % 2
                    pool.wait_ge(g_belo, g + 1)
                    nc.gpsimd.tensor_tensor(HBlo[:, j2, :, 0:C], HT[:, j].bitcast(F32),
                                            Belo[:, j2].unsqueeze(2).to_broadcast([P, CT, C]), ALU.mult).then_inc(g_hb, 1)
                if live(t, 2):
                    g, j2 = t + 2, k % 2
                    pool.wait_ge(a_ht, g + 1)
                    nc.gpsimd.tensor_tensor(cnt1[:, j2], cnt[:, j2], tiny[:], ALU.add).then_inc(g_cnt, 1)
                    pool.wait_ge(g_cnt, g + 1)
                    nc.gpsimd.tensor_tensor(Be[:, j2], cnt1[:, j2], half_pow[:, 0:CT], ALU.pow).then_inc(g_be, 1)
                    pool.wait_ge(g_be, g + 1)
                    nc.gpsimd.tensor_tensor(Behi[:, j2], Be[:, j2], ones_sq[:, 0:CT], ALU.mult).then_inc(g_behi, 1)
                if live(t, 1):
                    g, j, j2 = t + 1, (k + 1) % 4, (k + 1) % 2
                    nc.gpsimd.tensor_tensor(xlo[:, j2], x_t[:, j], xhi[:, j2].bitcast(F32), ALU.subtract).then_inc(g_x, 1)
                if live(t, 3):
                    g, j, j2 = t + 3, (k + 3) % 4, (k + 1) % 2
                    pool.wait_ge(s_wd[j], 2 * loaded(g, j))
                    if live(g, -2):
                        pool.wait_ge(p_s, g - 1)
                    nc.gpsimd.tensor_tensor(HBhi[:, j2, :, C], wd_t[:, j, 0], ones_sq[:, 0:CT], ALU.mult).then_inc(g_wc, 1)
                if live(t, -1):
                    g, j2 = t - 1, (k + 1) % 2
                    pool.wait_ge(v_agy, g + 1)
                    nc.gpsimd.tensor_tensor(ve_y[:, j2], ag_y[:, j2, :, 1], eps[:], ALU.add).then_inc(g_ey, 1)
                    nc.gpsimd.tensor_tensor(nm_y[:, j2], ag_y[:, j2, :, 0], minus[:], ALU.mult)
                    pool.wait_ge(g_ey, g + 1)
                    nc.gpsimd.tensor_tensor(rs_y[:, j2], ve_y[:, j2], half_pow[:, 2:4], ALU.pow).then_inc(g_ry, 1)
                    pool.wait_ge(g_ry, g + 1)
                    nc.gpsimd.tensor_tensor(nb_y[:, j2], nm_y[:, j2], rs_y[:, j2], ALU.mult).then_inc(g_nby, 1)
                if live(t, 1):
                    g, j, j2 = t + 1, (k + 1) % 4, (k + 1) % 2
                    pool.wait_ge(v_sc, g + 1)
                    nc.gpsimd.tensor_tensor(sc[:, j], sc_in[:, j2], half_pow[:], ALU.pow).then_inc(g_sc, 1)
                if live(t, -3):
                    g, j2 = t - 3, (k + 1) % 2
                    pool.wait_ge(v_ago, g + 1)
                    nc.gpsimd.tensor_tensor(ve_o[:, j2], ag_o[:, j2, :, 1], eps[:], ALU.add).then_inc(g_eo, 1)
                    nc.gpsimd.tensor_tensor(nm_o[:, j2], ag_o[:, j2, :, 0], minus[:], ALU.mult)
                    pool.wait_ge(g_eo, g + 1)
                    nc.gpsimd.tensor_tensor(rs_o[:, j2], ve_o[:, j2], half_pow[:, 2:4], ALU.pow).then_inc(g_ro, 1)
                    pool.wait_ge(g_ro, g + 1)
                    nc.gpsimd.tensor_tensor(nb_o[:, j2], nm_o[:, j2], rs_o[:, j2], ALU.mult).then_inc(g_nbo, 1)
                if live(t, 1):
                    g, j, j2 = t + 1, (k + 1) % 4, (k + 1) % 2
                    pool.wait_ge(g_sc, g + 1)
                    nc.gpsimd.tensor_tensor(Dn[:, j], sc[:, j, 0:2], sc_mask[:, j2], ALU.mult).then_inc(g_dn, 1)
                if live(t, 0):
                    g, j2 = t, k % 2
                    pool.wait_ge(v_agv, g + 1)
                    nc.gpsimd.tensor_tensor(ve_v[:, j2], ag_v[:, j2, :, 1], eps[:], ALU.add).then_inc(g_ev, 1)
                    pool.wait_ge(g_ev, g + 1)
                    nc.gpsimd.tensor_tensor(rs_v[:, j2], ve_v[:, j2], half_pow[:, 2:4], ALU.pow).then_inc(g_rv, 1)
                if live(t, -2):
                    g, j, j2 = t - 2, (k + 2) % 4, k % 2
                    pool.wait_ge(a_th, g + 1)
                    nc.gpsimd.tensor_tensor(res[:, j2], x1[:, j], th[:, j2], ALU.add).then_inc(g_res, 1)

            run_slots(pool, slot)

        @block.scalar
        def _(act):
            def slot(t, k):
                if live(t, -2):
                    g, j2 = t - 2, k % 2
                    act.wait_ge(p_z, g + 1)
                    nc.scalar.copy(zhi[:, j2].rearrange("p t c -> p (t c)"), ps[:, Z_BANK]).then_inc(a_z, 1)
                if live(t, 1):
                    g, j, j2 = t + 1, (k + 1) % 4, (k + 1) % 2
                    act.wait_ge(g_behi, g + 1)
                    for e in range(CT):
                        last = nc.scalar.activation(HBhi[:, j2, e, 0:C], HT[:, j, e].bitcast(F32), ACT.Copy,
                                                    scale=Behi[:, j2, e:e + 1].bitcast(F32))
                    last.then_inc(a_hb, 1)
                if live(t, 0):
                    g, j2 = t, k % 2
                    act.wait_ge(v_z1, g + 1)
                    nc.scalar.activation(v[:, j2, 1], z[:, j2, 1], ACT.Relu).then_inc(a_relu1, 1)
                if live(t, 2):
                    g, j, j2 = t + 2, (k + 2) % 4, k % 2
                    act.wait_ge(p_ht, g + 1)
                    for e in range(CT):
                        last = nc.scalar.activation(HT[:, j, e], psHT[:, e * C:(e + 1) * C], ACT.Copy,
                                                    accum_out=cnt[:, j2, e:e + 1])
                    last.then_inc(a_ht, 1)
                if live(t, 0):
                    g, j2 = t, k % 2
                    act.wait_ge(v_z0, g + 1)
                    nc.scalar.activation(v[:, j2, 0], z[:, j2, 0], ACT.Relu).then_inc(a_relu0, 1)
                if live(t, 1):
                    g, j = t + 1, (k + 1) % 4
                    act.wait_ge(p_s, g + 1)
                    nc.scalar.copy(Shi[:, j], ps[:, S_BANK[0]:S_BANK[0] + 2, 0:C]).then_inc(a_s, 1)
                if live(t, 0):
                    g, j2 = t, k % 2
                    act.wait_ge(p_v1, g + 1)
                    nc.scalar.copy(vhi[:, j2, 2:4].rearrange("p t c -> p (t c)"), ps[:, V_BANK[1]]).then_inc(a_v1, 1)
                if live(t, 0):
                    g, j2 = t, k % 2
                    act.wait_ge(p_v0, g + 1)
                    nc.scalar.copy(vhi[:, j2, 0:2].rearrange("p t c -> p (t c)"), ps[:, V_BANK[0]]).then_inc(a_v0, 1)
                if live(t, -1):
                    g, j, j2 = t - 1, (k + 3) % 4, (k + 1) % 2
                    act.wait_ge(g_nby, g + 1)
                    for c in range(CT):
                        last = nc.scalar.activation(x1[:, j, c], y[:, j2, c], ACT.Identity, bias=nb_y[:, j2, c:c + 1],
                                                    scale=rs_y[:, j2, c:c + 1])
                    last.then_inc(a_x1, 1)
                if live(t, 1):
                    g, j2 = t + 1, (k + 1) % 2
                    act.wait_ge(p_u, g + 1)
                    nc.scalar.copy(uhi[:, j2].rearrange("p t c -> p (t c)"), ps[:, U_BANK]).then_inc(a_u, 1)
                if live(t, -1):
                    g, j, j2 = t - 1, (k + 3) % 4, (k + 1) % 2
                    act.wait_ge(a_x1, g + 1)
                    for c in range(CT):
                        last = nc.scalar.activation(xdhi[:, j2, c], x1[:, j, c], ACT.Copy, scale=sc[:, j, 2 + c:3 + c])
                    last.then_inc(a_xd, 1)
                if live(t, 2):
                    g, j, j2 = t + 2, (k + 2) % 4, k % 2
                    act.wait_ge(s_x[j], loaded(g, j))
                    nc.scalar.copy(xhi[:, j2], x_t[:, j]).then_inc(a_x, 1)
                if live(t, -2):
                    g, j2 = t - 2, k % 2
                    act.wait_ge(v_a, g + 1)
                    nc.scalar.activation(th[:, j2], a_pre[:, j2], ACT.Tanh).then_inc(a_th, 1)
                if live(t, -3):
                    g, j2 = t - 3, (k + 1) % 2
                    act.wait_ge(g_nbo, g + 1)
                    if live(g, -2):
                        act.wait_ge(s_out[j2], (g - j2) * 8)
                    for c in range(CT):
                        last = nc.scalar.activation(out_t[:, j2, c], res[:, j2, c], ACT.Identity,
                                                    bias=nb_o[:, j2, c:c + 1], scale=rs_o[:, j2, c:c + 1])
                    last.then_inc(a_o, 1)
                if live(t, 0):
                    g, j2 = t, k % 2
                    act.wait_ge(v_w, g + 1)
                    nc.scalar.copy(hwhi[:, j2], hw[:, j2]).then_inc(a_w, 1)

            run_slots(act, slot)

        @block.vector
        def _(dve):
            dve.wait_ge(s_w, 8 * 16)
            dve.wait_ge(s_id, 12)
            for h in range(HT_):
                last = nc.vector.tensor_scalar(beta_sq[:, h], ones_sq[:], bcol[:, h:h + 1], None, ALU.mult)
            last.then_inc(s_cdve, 1)
            nc.vector.tensor_copy(Whi[:], Wn[:]).then_inc(s_wend, 1)
            dve.wait_ge(s_wps, 1)
            nc.vector.tensor_copy(W1hi[:], ps[:, 0:2, 0:DH]).then_inc(s_wend, 1)
            for q in range(2):
                nc.vector.tensor_copy(W2T[:, 2 * q:2 * q + 2].rearrange("p t c -> p (t c)"),
                                      ps[:, 2 + q]).then_inc(s_wsb, 1)
            for q in range(2):
                for h in range(2):
                    last = nc.vector.tensor_scalar(G[:, 2 * q + h], ps[:, 2 + q, h * D:(h + 1) * D],
                                                   gcol[:, 2 * q + h:2 * q + h + 1], None, ALU.mult)
            last.then_inc(s_wsb, 1)
            dve.wait_ge(s_wend, 2)
            nc.vector.tensor_tensor(Wlo[:], Wn[:], Whi[:].bitcast(F32), ALU.subtract).then_inc(s_wend, 1)
            nc.vector.tensor_tensor(W1lo[:], ps[:, 0:2, 0:DH], W1hi[:].bitcast(F32), ALU.subtract).then_inc(s_wend, 1)
            dve.wait_ge(s_gps, 1)
            nc.vector.tensor_copy(bW_b[:], ps[:, 4, 0:D])
            nc.vector.tensor_copy(b1_b[:], ps[:, 6, 0:DH])
            for c in range(CT):
                nc.vector.tensor_copy(b2_b[:, c], ps[:, 7, 0:D])
            nc.vector.tensor_copy(bL_b[:], ps[:, 7, D:2 * D])
            nc.vector.tensor_copy(gmean[:], ps[:, 5, 0:D]).then_inc(s_gsb, 1)
            dve.wait_ge(s_gsb, 1)
            for h in range(HT_):
                last = nc.vector.tensor_tensor(Gc[:, h], G[:, h], gmean[:], ALU.subtract)
            last.then_inc(s_gsb, 1)
            dve.wait_ge(s_gsb, 2)
            nc.vector.tensor_copy(Ghi[:], Gc[:]).then_inc(s_gsb, 1)
            dve.wait_ge(s_gsb, 3)
            nc.vector.tensor_tensor(Glo[:], Gc[:], Ghi[:].bitcast(F32), ALU.subtract).then_inc(s_wend, 1)

            def slot(t, k):
                if live(t, -2):
                    g, j, j2 = t - 2, (k + 2) % 4, k % 2
                    dve.wait_ge(a_xd, g + 1)
                    for c in range(CT):
                        last = nc.vector.scalar_tensor_tensor(xdlo[:, j2, c], x1[:, j, c], sc[:, j, 2 + c:3 + c],
                                                              xdhi[:, j2, c].bitcast(F32), ALU.mult, ALU.subtract)
                    last.then_inc(v_xd, 1)
                if live(t, -1):
                    g, j2 = t - 1, (k + 1) % 2
                    dve.wait_ge(p_w, g + 1)
                    dve.wait_ge(g_rv, g + 1)
                    for c in range(CT):
                        last = nc.vector.scalar_tensor_tensor(hw[:, j2, c], ps[:, W_BANK, c * D:(c + 1) * D],
                                                              rs_v[:, j2, c:c + 1], bW_b[:], ALU.mult, ALU.add)
                    last.then_inc(v_w, 1)
                if live(t, -1):
                    g, j, j2 = t - 1, (k + 3) % 4, (k + 1) % 2
                    nc.vector.scalar_tensor_tensor(xb[:, j2], x_t[:, j], 2.0, b2_b[:], ALU.mult, ALU.add).then_inc(v_xb, 1)
                if live(t, 0):
                    g, j, j2 = t, k, k % 2
                    dve.wait_ge(p_r1, g + 1)
                    dve.wait_ge(g_dn, g + 1)
                    nc.vector.scalar_tensor_tensor(z[:, j2, 1], ps[:, R_BANK[1], 0:DH], Dn[:, j, 1:2],
                                                   b1_b[:], ALU.mult, ALU.add).then_inc(v_z1, 1)
                if live(t, -3):
                    g, j2 = t - 3, (k + 1) % 2
                    dve.wait_ge(g_res, g + 1)
                    for c in range(CT):
                        last = nc.vector.bn_stats(bn_o[:, c], res[:, j2, c])
                    last.then_inc(v_bno, 1)
                if live(t, -2):
                    g, j2 = t - 2, k % 2
                    dve.wait_ge(a_z, g + 1)
                    nc.vector.tensor_tensor(zlo[:, j2].rearrange("p t c -> p (t c)"), ps[:, Z_BANK],
                                            zhi[:, j2].rearrange("p t c -> p (t c)").bitcast(F32),
                                            ALU.subtract).then_inc(v_z, 1)
                if live(t, 3):
                    g, j, j2 = t + 3, (k + 3) % 4, (k + 1) % 2
                    dve.wait_ge(s_adj[j], loaded(g, j))
                    if live(g, -2):
                        dve.wait_ge(p_ht, g - 1)
                    nc.vector.tensor_scalar(Hb[:, j2], adj_t[:, j], 0.0, None, ALU.not_equal).then_inc(v_h, 1)
                if live(t, 0):
                    g, j, j2 = t, k, k % 2
                    dve.wait_ge(p_r0, g + 1)
                    nc.vector.scalar_tensor_tensor(z[:, j2, 0], ps[:, R_BANK[0], 0:DH], Dn[:, j, 0:1],
                                                   b1_b[:], ALU.mult, ALU.add).then_inc(v_z0, 1)
                if live(t, 0):
                    g, j2 = t, k % 2
                    dve.wait_ge(a_relu1, g + 1)
                    nc.vector.bn_stats(bn_v[:, 1], v[:, j2, 1]).then_inc(v_bnv1, 1)
                if live(t, -1):
                    g, j, j2 = t - 1, (k + 3) % 4, (k + 1) % 2
                    dve.wait_ge(p_y, g + 1)
                    dve.wait_ge(v_xb, g + 1)
                    if live(t, -3):
                        dve.wait_ge(v_bno, t - 2)
                    for c in range(CT):
                        last = nc.vector.scalar_tensor_tensor(y[:, j2, c], ps[:, Y_BANK, c * D:(c + 1) * D],
                                                              Dn[:, j, c:c + 1], xb[:, j2, c], ALU.mult, ALU.add)
                    last.then_inc(v_y, 1)
                if live(t, -3):
                    g, j2 = t - 3, (k + 1) % 2
                    if not live(t, -1):
                        dve.wait_ge(v_bno, g + 1)
                    for c in range(CT):
                        last = nc.vector.bn_aggr(ag_o[:, j2, c], bn_o[:, c])
                    last.then_inc(v_ago, 1)
                if live(t, -1):
                    g, j2 = t - 1, (k + 1) % 2
                    dve.wait_ge(v_y, g + 1)
                    for c in range(CT):
                        last = nc.vector.bn_stats(bn_y[:, c], y[:, j2, c])
                    last.then_inc(v_bny, 1)
                if live(t, 1):
                    g, j, j2 = t + 1, (k + 1) % 4, (k + 1) % 2
                    dve.wait_ge(a_s, g + 1)
                    if live(t, -1):
                        dve.wait_ge(v_bny, t)
                    d_col = ps[:, S_BANK[0]:S_BANK[0] + 2, C]
                    rc_col = ps[:, S_BANK[0]:S_BANK[0] + 2, C + 1]
                    nc.vector.tensor_scalar(sc_in[:, j2, 0:2], d_col, TINY, None, ALU.max)
                    nc.vector.tensor_scalar(sc_mask[:, j2], d_col, 0.0, None, ALU.is_gt)
                    nc.vector.scalar_tensor_tensor(sc_in[:, j2, 2:4], wd_t[:, j, 1], 0.0, rc_col,
                                                   ALU.is_equal, ALU.add).then_inc(v_sc, 1)
                if live(t, -1):
                    g, j2 = t - 1, (k + 1) % 2
                    if not live(t, 1):
                        dve.wait_ge(v_bny, g + 1)
                    for c in range(CT):
                        last = nc.vector.bn_aggr(ag_y[:, j2, c], bn_y[:, c])
                    last.then_inc(v_agy, 1)
                if live(t, 1):
                    g, j = t + 1, (k + 1) % 4
                    nc.vector.tensor_tensor(Slo[:, j], ps[:, S_BANK[0]:S_BANK[0] + 2, 0:C], Shi[:, j].bitcast(F32),
                                            ALU.subtract).then_inc(v_s, 1)
                if live(t, 0):
                    g, j2 = t, k % 2
                    dve.wait_ge(a_v1, g + 1)
                    nc.vector.tensor_tensor(vlo[:, j2, 2:4].rearrange("p t c -> p (t c)"), ps[:, V_BANK[1]],
                                            vhi[:, j2, 2:4].rearrange("p t c -> p (t c)").bitcast(F32),
                                            ALU.subtract).then_inc(v_v1, 1)
                if live(t, 0):
                    g, j2 = t, k % 2
                    dve.wait_ge(a_v0, g + 1)
                    nc.vector.tensor_tensor(vlo[:, j2, 0:2].rearrange("p t c -> p (t c)"), ps[:, V_BANK[0]],
                                            vhi[:, j2, 0:2].rearrange("p t c -> p (t c)").bitcast(F32),
                                            ALU.subtract).then_inc(v_v0, 1)
                if live(t, 0):
                    g, j2 = t, k % 2
                    nc.vector.bn_stats(bn_v[:, 0], v[:, j2, 0]).then_inc(v_bnv0, 1)
                if live(t, 1):
                    g, j = t + 1, (k + 1) % 4
                    if live(t, 0):
                        dve.wait_ge(v_bnv0, t + 1)
                    for c in range(CT):
                        blk = HT[:, j, c, c * P:(c + 1) * P]
                        last = nc.vector.tensor_tensor(blk, blk.bitcast(F32), ident[:], ALU.max)
                    last.then_inc(v_at, 1)
                if live(t, 0):
                    g, j2 = t, k % 2
                    if not live(t, 1):
                        dve.wait_ge(v_bnv0, g + 1)
                    for c in range(CT):
                        last = nc.vector.bn_aggr(ag_v[:, j2, c], bn_v[:, c])
                    last.then_inc(v_agv, 1)
                if live(t, -2):
                    g, j, j2 = t - 2, (k + 2) % 4, k % 2
                    dve.wait_ge(p_a, g + 1)
                    for c in range(CT):
                        last = nc.vector.scalar_tensor_tensor(a_pre[:, j2, c], ps[:, A_BANK, c * D:(c + 1) * D],
                                                              sc[:, j, 2 + c:3 + c], bL_b[:], ALU.mult, ALU.add)
                    last.then_inc(v_a, 1)
                if live(t, 1):
                    g, j2 = t + 1, (k + 1) % 2
                    dve.wait_ge(a_u, g + 1)
                    nc.vector.tensor_tensor(ulo[:, j2].rearrange("p t c -> p (t c)"), ps[:, U_BANK],
                                            uhi[:, j2].rearrange("p t c -> p (t c)").bitcast(F32),
                                            ALU.subtract).then_inc(v_u, 1)

            run_slots(dve, slot)

        @block.tensor
        def _(pe):
            def product(out_ap, pairs, kt):
                n, total = 0, len(pairs) * kt
                for left, right in pairs:
                    for q in range(kt):
                        last = nc.tensor.matmul(out_ap, left(q), right(q), start=(n == 0), stop=(n == total - 1))
                        n += 1
                return last

            def three(lhi, llo, rhi, rlo):
                return [(lhi, rhi), (lhi, rlo), (llo, rhi)]

            pe.wait_ge(s_w, 8 * 16)
            pe.wait_ge(s_id, 12)
            for d in range(DT):
                for h in range(HT_):
                    nc.tensor.transpose(ps[:, d, h * P:(h + 1) * P], W1n[:, h, d * P:(d + 1) * P], ident[:])
            for h in range(HT_):
                for o in range(DT):
                    q = (h % 2) * D + o * P
                    last = nc.tensor.transpose(ps[:, 2 + h // 2, q:q + P], W2n[:, o, h * P:(h + 1) * P], ident[:])
            last.then_inc(s_wps, 1)
            nc.tensor.matmul(ps[:, 6, 0:DH], ones_row[:], rows[0:1, 0:DH], start=True, stop=True)
            nc.tensor.matmul(ps[:, 7, 0:2 * D], ones_row[:], rows[0:1, DH:DH + 2 * D], start=True, stop=True)
            pe.wait_ge(s_cdve, 1)
            pe.wait_ge(s_wsb, 3)
            product(ps[:, 4, 0:D], [(lambda q: beta_sq[:, q], lambda q: W2T[:, q])], HT_)
            product(ps[:, 5, 0:D], [(lambda q: mean_w[:], lambda q: G[:, q])], HT_).then_inc(s_gps, 1)
            pe.wait_ge(s_wend, 5)

            def slot(t, k):
                if live(t, 1):
                    g, j2 = t + 1, (k + 1) % 2
                    pe.wait_ge(v_h, g + 1)
                    if live(g, -1):
                        pe.wait_ge(a_ht, g)
                    for e in range(CT):
                        for c in range(CT):
                            last = nc.tensor.transpose(psHT[:, e * C + c * P:e * C + (c + 1) * P],
                                                       Hb[:, j2, c, e * P:(e + 1) * P], ident_bf[:])
                    last.then_inc(p_ht, 1)
                if live(t, -1):
                    g, j, j2 = t - 1, (k + 3) % 4, (k + 1) % 2
                    pe.wait_ge(g_x, g + 1)
                    pe.wait_ge(v_s, g + 1)
                    for d in range(DT):
                        cs = slice(d * P, (d + 1) * P)
                        last = product(ps[:, U_BANK, d * C:(d + 1) * C],
                                       three(lambda q: xhi[:, j2, q, cs], lambda q: xlo[:, j2, q, cs],
                                             lambda q: Shi[:, j, q], lambda q: Slo[:, j, q]), CT)
                    last.then_inc(p_u, 1)
                if live(t, -2):
                    g, j2 = t - 2, k % 2
                    pe.wait_ge(v_v0, g + 1)
                    for c in range(CT):
                        cs = slice(c * P, (c + 1) * P)
                        last = product(ps[:, W_BANK, c * D:(c + 1) * D],
                                       three(lambda q: vhi[:, j2, q, cs], lambda q: vlo[:, j2, q, cs],
                                             lambda q: Ghi[:, q], lambda q: Glo[:, q]), HT_)
                    last.then_inc(p_w, 1)
                if live(t, -1):
                    g, j2 = t - 1, (k + 1) % 2
                    pe.wait_ge(v_u, g + 1)
                    product(ps[:, R_BANK[1], 0:DH],
                            three(lambda q: uhi[:, j2, q, P:2 * P], lambda q: ulo[:, j2, q, P:2 * P],
                                  lambda q: W1hi[:, q], lambda q: W1lo[:, q]), DT).then_inc(p_r1, 1)
                if live(t, -3):
                    g, j, j2 = t - 3, (k + 1) % 4, (k + 1) % 2
                    pe.wait_ge(v_xd, g + 1)
                    for d in range(DT):
                        cs = slice(d * P, (d + 1) * P)
                        last = product(ps[:, Z_BANK, d * C:(d + 1) * C],
                                       [(lambda q: xdhi[:, j2, q, cs], lambda q: HT[:, j, q]),
                                        (lambda q: xdlo[:, j2, q, cs], lambda q: HT[:, j, q])], CT)
                    last.then_inc(p_z, 1)
                if live(t, -1):
                    g, j2 = t - 1, (k + 1) % 2
                    product(ps[:, R_BANK[0], 0:DH],
                            three(lambda q: uhi[:, j2, q, 0:P], lambda q: ulo[:, j2, q, 0:P],
                                  lambda q: W1hi[:, q], lambda q: W1lo[:, q]), DT).then_inc(p_r0, 1)
                if live(t, -2):
                    g, j, j2 = t - 2, (k + 2) % 4, k % 2
                    pe.wait_ge(g_w, g + 1)
                    for c in range(CT):
                        cs = slice(c * P, (c + 1) * P)
                        last = product(ps[:, Y_BANK, c * D:(c + 1) * D],
                                       three(lambda q: Shi[:, j, q, cs], lambda q: Slo[:, j, q, cs],
                                             lambda q: hwhi[:, j2, q], lambda q: hwlo[:, j2, q]), CT)
                    last.then_inc(p_y, 1)
                if live(t, 0):
                    g, j, j2 = t, k, k % 2
                    pe.wait_ge(a_hb, g + 1)
                    pe.wait_ge(g_hb, g + 1)
                    if live(g, -3):
                        pe.wait_ge(v_z, g - 2)
                    elif live(g, -1):
                        pe.wait_ge(v_s, g)
                    for c in range(CT):
                        cs = slice(c * P, (c + 1) * P)
                        last = product(ps[:, S_BANK[c], 0:C + 2],
                                       [(lambda q: HT[:, j, q, cs], lambda q: HBhi[:, j2, q]),
                                        (lambda q: HT[:, j, q, cs], lambda q: HBlo[:, j2, q])], CT)
                    last.then_inc(p_s, 1)
                if live(t, -1):
                    g, j2 = t - 1, (k + 1) % 2
                    pe.wait_ge(a_relu0, g + 1)
                    for h in range(2):
                        for c in range(CT):
                            last = nc.tensor.transpose(ps[:, V_BANK[1], h * C + c * P:h * C + (c + 1) * P],
                                                       v[:, j2, c, (2 + h) * P:(2 + h + 1) * P], ident[:])
                    last.then_inc(p_v1, 1)
                if live(t, -1):
                    g, j2 = t - 1, (k + 1) % 2
                    for h in range(2):
                        for c in range(CT):
                            last = nc.tensor.transpose(ps[:, V_BANK[0], h * C + c * P:h * C + (c + 1) * P],
                                                       v[:, j2, c, (h) * P:(h + 1) * P], ident[:])
                    last.then_inc(p_v0, 1)
                if live(t, -3):
                    g, j2 = t - 3, (k + 1) % 2
                    pe.wait_ge(v_z, g + 1)
                    for c in range(CT):
                        cs = slice(c * P, (c + 1) * P)
                        last = product(ps[:, A_BANK, c * D:(c + 1) * D],
                                       three(lambda q: zhi[:, j2, q, cs], lambda q: zlo[:, j2, q, cs],
                                             lambda q: Whi[:, q], lambda q: Wlo[:, q]), DT)
                    last.then_inc(p_a, 1)

            run_slots(pe, slot)


_INS = ['x', 'adj', 'L0_gnn_W1', 'L0_gnn_b1', 'L0_gnn_gamma', 'L0_gnn_beta', 'L0_gnn_W2', 'L0_gnn_b2',
        'L1_gnn_W', 'L1_gnn_b']


def kernel(**inputs):
    import numpy as _np
    import concourse.bacc as _bacc
    from concourse import mybir as _mybir
    from concourse.bass_utils import run_bass_kernel_spmd as _run

    nc = _bacc.Bacc("TRN2", target_bir_lowering=False, num_devices=1)
    arrays, args = {}, []
    for name in _INS:
        a = _np.ascontiguousarray(inputs[name])
        arrays[f"in_{name}_dram"] = a
        args.append(nc.dram_tensor(f"in_{name}_dram", a.shape, _mybir.dt.from_np(a.dtype), kind="ExternalInput").ap())
    shape = arrays["in_x_dram"].shape
    out = nc.dram_tensor("out_0_dram", shape, _mybir.dt.from_np(_np.dtype("float32")), kind="ExternalOutput").ap()
    bass_resnorm_graph_layers(nc, *args, out)
    r = _run(nc, [arrays], core_ids=[0])
    return r.results[0]["out_0_dram"]
```

```python
import numpy as np
import concourse.bass as bass
from concourse import mybir
from contextlib import ExitStack

F32 = mybir.dt.float32
F32R = mybir.dt.float32r
BF16 = mybir.dt.bfloat16
ALU = mybir.AluOpType
ACT = mybir.ActivationFunctionType

EPS = 1e-5
TINY = 1.2e-38
AHEAD, BEHIND = 4, 4
PEELED = 6
UNROLL = 4


def bass_resnorm_graph_layers(nc, x, adj, W1, b1, gamma, beta, W2, b2, W, b, out):
    NG, C, D = x.shape
    DH = W1.shape[0]
    P = 128
    CT, DT, HT_ = C // P, D // P, DH // P
    assert CT == 2 and DT == 2 and HT_ == 4

    LOOP_FROM = PEELED
    LOOP_TO = (NG - AHEAD - LOOP_FROM) // UNROLL * UNROLL + LOOP_FROM
    FIRST, LAST = -AHEAD, NG - 1 + BEHIND

    def live(t, off):
        return not isinstance(t, int) or 0 <= t + off < NG

    def once(t, at, step):
        if isinstance(t, int) and t == at:
            step()

    def run_slots(eng, slot):
        for t in range(FIRST, LOOP_FROM):
            slot(t, t % UNROLL)
        with eng.Fori(LOOP_FROM, LOOP_TO - UNROLL + 1, UNROLL) as t0:
            for k in range(UNROLL):
                slot(t0 + k, (LOOP_FROM + k) % UNROLL)
        for t in range(LOOP_TO, LAST + 1):
            slot(t, t % UNROLL)

    def diag_blocks(m):
        flat = m.rearrange("p t c -> p (t c)")
        return bass.AP(tensor=flat.tensor, offset=flat.offset, ap=[list(flat.ap[0]), [C + P, CT], [1, P]])

    def loaded(g, j):
        return (g - j) * 4 + 16

    ctx = ExitStack()
    with ctx:
        def sb(name, shape, dt=F32):
            return ctx.enter_context(nc.sbuf_tensor(name, shape, dt))

        def sem(name):
            return ctx.enter_context(nc.semaphore(name))

        ident_bf = sb("ident_bf", [P, P], BF16)
        ident = sb("ident", [P, P])
        tiny = sb("tiny", [P, CT])
        eps = sb("eps", [P, CT])
        minus = sb("minus", [P, CT])
        half_pow = sb("half_pow", [P, 4])
        Wn = sb("Wn", [P, DT, D])
        ones_sq = sb("ones_sq", [P, P])
        g_mean = sb("g_mean", [P, DT])
        g_sum = sb("g_sum", [P, DT])
        b_sum = sb("b_sum", [P, DT])
        W1hi, W1lo = sb("W1hi", [P, DT, DH], F32R), sb("W1lo", [P, DT, DH], F32R)
        Ghi, Glo = sb("Ghi", [P, HT_, D], F32R), sb("Glo", [P, HT_, D], F32R)
        Whi, Wlo = sb("Whi", [P, DT, D], F32R), sb("Wlo", [P, DT, D], F32R)
        b1_b = sb("b1_b", [P, DH])
        b2_b = sb("b2_b", [P, CT, D])
        bL_b = sb("bL_b", [P, D])
        bW_b = sb("bW_b", [P, D])

        adj_t = sb("adj_t", [P, 4, CT, C])
        x_t = sb("x_t", [P, 4, CT, D])
        wd_t = sb("wd_t", [P, 4, 2, CT])
        Hb = sb("Hb", [P, 2, CT, C], BF16)
        HT = sb("HT", [P, 4, CT, C], F32R)
        cnt = sb("cnt", [P, 2, CT])
        cnt1 = sb("cnt1", [P, 2, CT])
        Be = sb("Be", [P, 2, CT])
        Behi = sb("Behi", [P, 2, CT], F32R)
        Belo = sb("Belo", [P, 2, CT])
        HBhi, HBlo = sb("HBhi", [P, 2, CT, C + 2], F32R), sb("HBlo", [P, 2, CT, C + 2], F32R)
        xhi, xlo = sb("xhi", [P, 2, CT, D], F32R), sb("xlo", [P, 2, CT, D], F32R)
        Shi, Slo = sb("Shi", [P, 4, CT, C], F32R), sb("Slo", [P, 4, CT, C], F32R)
        sc_in = sb("sc_in", [P, 2, 4])
        sc_mask = sb("sc_mask", [P, 2, CT])
        sc = sb("sc", [P, 4, 4])
        Dn = sb("Dn", [P, 4, CT])
        uhi, ulo = sb("uhi", [P, 2, DT, C], F32R), sb("ulo", [P, 2, DT, C], F32R)
        z = sb("z", [P, 2, CT, DH])
        v = sb("v", [P, 2, CT, DH])
        W1n = z[:, 0].rearrange("p t (u d) -> p (t u) d", d=D)
        W2n = z[:, 1]
        bn_v, ag_v, rs_v = sb("bn_v", [P, 2, CT, 6]), sb("ag_v", [P, 2, CT, 2]), sb("rs_v", [P, 2, CT])
        ve_v = sb("ve_v", [P, 2, CT])
        vhi, vlo = sb("vhi", [P, 2, HT_, C], F32R), sb("vlo", [P, 2, HT_, C], F32R)
        hw = sb("hw", [P, 2, CT, D])
        hwhi, hwlo = sb("hwhi", [P, 2, CT, D], F32R), sb("hwlo", [P, 2, CT, D], F32R)
        xb = sb("xb", [P, 2, CT, D])
        y = sb("y", [P, 2, CT, D])
        bn_y, ag_y, rs_y = sb("bn_y", [P, 2, CT, 6]), sb("ag_y", [P, 2, CT, 2]), sb("rs_y", [P, 2, CT])
        ve_y, nm_y, nb_y = (sb(f"{n}_y", [P, 2, CT]) for n in ("ve", "nm", "nb"))
        x1 = sb("x1", [P, 4, CT, D])
        xdhi, xdlo = sb("xdhi", [P, 2, CT, D], F32R), sb("xdlo", [P, 2, CT, D], F32R)
        zhi, zlo = sb("zhi", [P, 2, DT, C], F32R), sb("zlo", [P, 2, DT, C], F32R)
        a_pre = sb("a_pre", [P, 2, CT, D])
        th = sb("th", [P, 2, CT, D])
        res = sb("res", [P, 2, CT, D])
        bn_o, ag_o, rs_o = sb("bn_o", [P, 2, CT, 6]), sb("ag_o", [P, 2, CT, 2]), sb("rs_o", [P, 2, CT])
        ve_o, nm_o, nb_o = (sb(f"{n}_o", [P, 2, CT]) for n in ("ve", "nm", "nb"))
        out_t = sb("out_t", [P, 2, CT, D])

        Gn, Bn = (buf[:].rearrange("p b t d -> p b (t d)") for buf in (th, out_t))
        gamma_b, beta_b = (x1[:, q].rearrange("p t d -> p (t d)") for q in range(2))
        b_sq = res[:, 0].rearrange("p t d -> p (t d)")[:, 0:2 * P].rearrange("p (o m) -> p o m", m=P)
        ps = ctx.enter_context(nc.psum_tensor("ps", [P, 8, 512], F32))
        R_BANK, V_BANK = (0, 1), (0, 7)
        S_BANK, U_BANK, Z_BANK = (2, 3), 1, 6
        Y_BANK, A_BANK, W_BANK, HT_BANK = 5, 4, 7, 1
        G_BANK, B_BANK = (4, 5), 6
        psHT = ps[:, HT_BANK, 0:C].bitcast(BF16)

        s_w1, s_w2, s_wb = sem("w1_in"), sem("w2_gamma_beta_in"), sem("w_and_biases_in")
        s_adj = [sem(f"adj_in{j}") for j in range(4)]
        s_x = [sem(f"x_in{j}") for j in range(4)]
        s_wd = [sem(f"wd_in{j}") for j in range(4)]
        s_out = [sem(f"out_stored{j}") for j in range(2)]
        s_id0, s_id = sem("ident_zeroed"), sem("consts_made")
        w1_ps, w1_hi, w1_lo = sem("w1t_in_psum"), sem("w1_hi"), sem("w1_lo")
        gb_n, gm_ready, g_c, b_c = sem("gamma_beta_products"), sem("g_mean_ready"), sem("g_centred"), sem("b_sum_spread")
        g_ps, b_ps, gg_hi, gg_lo, bw_in = sem("gt_in_psum"), sem("bw_in_psum"), sem("g_hi"), sem("g_lo"), sem("bw_ready")
        ww_hi, ww_lo = sem("w_weights_hi"), sem("w_weights_lo")
        p_ht, p_s, p_u, p_r0, p_r1 = (
            sem(n) for n in ("ht_in_psum", "s_in_psum", "u_in_psum", "r_in_psum0", "r_in_psum1"))
        p_v0, p_v1, p_w, p_y, p_z = (
            sem(n) for n in ("vt_in_psum0", "vt_in_psum1", "hw_in_psum", "y_in_psum", "z_in_psum"))
        p_a = sem("agg_in_psum")
        a_ht, a_hb, a_s, a_u, a_x = (
            sem(n) for n in ("ht_ready", "hb_hi", "s_hi", "u_hi", "x_hi"))
        a_relu0, a_relu1, a_v0, a_v1, a_w = (
            sem(n) for n in ("relu_done0", "relu_done1", "v_hi0", "v_hi1", "hw_hi"))
        a_xd, a_z, a_th, a_x1, a_o = (
            sem(n) for n in ("xd_hi", "z_hi", "tanh_done", "x1_ready", "out_ready"))
        v_h, v_sc, v_s, v_at, v_u = (
            sem(n) for n in ("h_ready", "scalars_read", "s_lo", "at_ready", "u_lo"))
        v_z0, v_z1, v_v0, v_v1, v_bnv0 = (
            sem(n) for n in ("z_biased0", "z_biased1", "v_lo0", "v_lo1", "v_bn0"))
        v_bnv1, v_agv, v_bny, v_agy, v_bno = (
            sem(n) for n in ("v_bn1", "v_stats", "y_bn", "y_stats", "o_bn"))
        v_ago, v_w, v_y, v_xd, v_z = (
            sem(n) for n in ("o_stats", "hw_biased", "y_summed", "xd_lo", "z_lo"))
        v_a, v_xb = (
            sem(n) for n in ("agg_biased", "xb_ready"))
        g_ev, g_ey, g_eo, g_cnt, g_be = (
            sem(n) for n in ("v_var_eps", "y_var_eps", "o_var_eps", "cnt_guarded", "be_inverse"))
        g_behi, g_belo, g_wc, g_hb, g_sc = (
            sem(n) for n in ("be_hi", "be_lo", "w_hi", "hb_lo", "scalars_powered"))
        g_dn, g_x, g_rv, g_w, g_ry = (
            sem(n) for n in ("dn_ready", "x_lo", "v_rstd", "hw_lo", "y_rstd"))
        g_nby, g_res, g_ro, g_nbo = (
            sem(n) for n in ("y_shift", "residual", "o_rstd", "o_shift"))

        block = ctx.enter_context(nc.Block())

        @block.sync
        def _(sp):
            def load_adj(g, j):
                sp.dma_start(adj_t[:, j], adj[g].rearrange("(t p) c -> p t c", p=P)).then_inc(s_adj[j], 16)

            def load_x(g, j):
                sp.dma_start(wd_t[:, j, 0], adj[g, 0].rearrange("(t p) -> p t", p=P),
                             allow_slow_non_contiguous=True).then_inc(s_wd[j], 16)
                sp.dma_start(wd_t[:, j, 1], diag_of(g), allow_slow_non_contiguous=True).then_inc(s_wd[j], 16)
                sp.dma_start(x_t[:, j], x[g].rearrange("(t p) c -> p t c", p=P)).then_inc(s_x[j], 16)

            def diag_of(g):
                flat = adj[g].rearrange("a b -> (a b)")
                return bass.AP(tensor=flat.tensor, offset=flat.offset, ap=[[C + 1, P], [(C + 1) * P, CT]])

            def row(vec, n, copies=1):
                return bass.AP(tensor=vec.tensor, offset=vec.offset, ap=[[0, P]] + [[0, copies]] * (copies > 1) + [[1, n]])

            def load_w1_w2():
                sp.dma_start(W1n, W1.rearrange("(t p) d -> p t d", p=P)).then_inc(s_w1, 16)
                sp.dma_start(W2n, W2.rearrange("(t p) d -> p t d", p=P)).then_inc(s_w2, 16)
                sp.dma_start(gamma_b, row(gamma, DH)).then_inc(s_w2, 16)
                sp.dma_start(beta_b, row(beta, DH)).then_inc(s_w2, 16)

            def load_rest():
                sp.dma_start(b1_b[:], row(b1, DH)).then_inc(s_wb, 16)
                sp.dma_start(b2_b[:], row(b2, D, CT)).then_inc(s_wb, 16)
                sp.dma_start(bL_b[:], row(b, D)).then_inc(s_wb, 16)
                sp.dma_start(Wn[:], W.rearrange("(t p) d -> p t d", p=P)).then_inc(s_wb, 16)

            def slot(t, k):
                once(t, -2, load_w1_w2)
                once(t, -1, load_rest)
                if live(t, 4):
                    g, j = t + 4, k
                    if live(g, -4):
                        sp.wait_ge(v_h, g - 3)
                    load_adj(g, j)
                if live(t, 4):
                    g, j = t + 4, k
                    if live(g, -4):
                        sp.wait_ge(v_xb, g - 3)
                    load_x(g, j)
                if live(t, -4):
                    g, j2 = t - 4, k % 2
                    sp.wait_ge(a_o, g + 1)
                    sp.dma_start(out[g].rearrange("(t p) c -> p t c", p=P), out_t[:, j2]).then_inc(s_out[j2], 16)

            run_slots(sp, slot)
            for j in range(2):
                sp.wait_ge(s_out[j], 16 * NG // 2)

        @block.gpsimd
        def _(pool):
            nc.gpsimd.memset(ident[:], 0.0).then_inc(s_id0, 1)
            nc.gpsimd.memset(half_pow[:, 0:2], -1.0).then_inc(s_id, 1)
            nc.gpsimd.memset(half_pow[:, 2:4], -0.5).then_inc(s_id, 1)
            nc.gpsimd.memset(ones_sq[:], 1.0).then_inc(s_id, 1)
            nc.gpsimd.memset(tiny[:], TINY).then_inc(s_id, 1)
            nc.gpsimd.memset(eps[:], EPS).then_inc(s_id, 1)
            nc.gpsimd.memset(minus[:], -1.0).then_inc(s_id, 1)
            nc.gpsimd.memset(HBhi[:, :, :, C + 1:C + 2].bitcast(F32), 1.0).then_inc(s_id, 1)
            nc.gpsimd.memset(HBlo[:, :, :, C + 1:C + 2].bitcast(F32), 0.0).then_inc(s_id, 1)
            pool.wait_ge(s_id0, 1)
            nc.gpsimd.affine_select(out=ident[:], in_=ident[:], compare_op=ALU.not_equal, fill=1.0, base=0,
                                    pattern=[[-1, P]], channel_multiplier=1).then_inc(s_id, 1)
            pool.wait_ge(s_id, 9)
            nc.gpsimd.tensor_copy(ident_bf[:], ident[:]).then_inc(s_id, 1)

            def slot(t, k):
                if live(t, 2):
                    g, j, j2 = t + 2, (k + 2) % 4, k % 2
                    pool.wait_ge(g_behi, g + 1)
                    nc.gpsimd.tensor_tensor(HBlo[:, j2, :, C], wd_t[:, j, 0], HBhi[:, j2, :, C].bitcast(F32), ALU.subtract)
                    nc.gpsimd.tensor_tensor(Belo[:, j2], Be[:, j2], Behi[:, j2].bitcast(F32), ALU.subtract).then_inc(g_belo, 1)
                if live(t, 2):
                    g, j, j2 = t + 2, (k + 2) % 4, k % 2
                    pool.wait_ge(g_belo, g + 1)
                    nc.gpsimd.tensor_tensor(HBlo[:, j2, :, 0:C], HT[:, j].bitcast(F32),
                                            Belo[:, j2].unsqueeze(2).to_broadcast([P, CT, C]), ALU.mult).then_inc(g_hb, 1)
                if live(t, -1):
                    g, j2 = t - 1, (k + 1) % 2
                    pool.wait_ge(v_agy, g + 1)
                    nc.gpsimd.tensor_tensor(ve_y[:, j2], ag_y[:, j2, :, 1], eps[:], ALU.add).then_inc(g_ey, 1)
                    nc.gpsimd.tensor_tensor(nm_y[:, j2], ag_y[:, j2, :, 0], minus[:], ALU.mult)
                    pool.wait_ge(g_ey, g + 1)
                    nc.gpsimd.tensor_tensor(rs_y[:, j2], ve_y[:, j2], half_pow[:, 2:4], ALU.pow).then_inc(g_ry, 1)
                    pool.wait_ge(g_ry, g + 1)
                    nc.gpsimd.tensor_tensor(nb_y[:, j2], nm_y[:, j2], rs_y[:, j2], ALU.mult).then_inc(g_nby, 1)
                if live(t, 0):
                    g, j2 = t, k % 2
                    pool.wait_ge(v_agv, g + 1)
                    nc.gpsimd.tensor_tensor(ve_v[:, j2], ag_v[:, j2, :, 1], eps[:], ALU.add).then_inc(g_ev, 1)
                    pool.wait_ge(g_ev, g + 1)
                    nc.gpsimd.tensor_tensor(rs_v[:, j2], ve_v[:, j2], half_pow[:, 2:4], ALU.pow).then_inc(g_rv, 1)
                if live(t, 1):
                    g, j, j2 = t + 1, (k + 1) % 4, (k + 1) % 2
                    pool.wait_ge(v_sc, g + 1)
                    nc.gpsimd.tensor_tensor(sc[:, j], sc_in[:, j2], half_pow[:], ALU.pow).then_inc(g_sc, 1)
                if live(t, 3):
                    g, j, j2 = t + 3, (k + 3) % 4, (k + 1) % 2
                    pool.wait_ge(s_wd[j], 2 * loaded(g, j))
                    nc.gpsimd.tensor_tensor(HBhi[:, j2, :, C], wd_t[:, j, 0], ones_sq[:, 0:CT], ALU.mult).then_inc(g_wc, 1)
                if live(t, 1):
                    g, j, j2 = t + 1, (k + 1) % 4, (k + 1) % 2
                    pool.wait_ge(g_sc, g + 1)
                    nc.gpsimd.tensor_tensor(Dn[:, j], sc[:, j, 0:2], sc_mask[:, j2], ALU.mult).then_inc(g_dn, 1)
                if live(t, 0):
                    g, j2 = t, k % 2
                    pool.wait_ge(a_w, g + 1)
                    nc.gpsimd.tensor_tensor(hwlo[:, j2], hw[:, j2], hwhi[:, j2].bitcast(F32), ALU.subtract).then_inc(g_w, 1)
                if live(t, 2):
                    g, j, j2 = t + 2, (k + 2) % 4, k % 2
                    pool.wait_ge(a_x, g + 1)
                    nc.gpsimd.tensor_tensor(xlo[:, j2], x_t[:, j], xhi[:, j2].bitcast(F32), ALU.subtract).then_inc(g_x, 1)
                if live(t, -2):
                    g, j, j2 = t - 2, (k + 2) % 4, k % 2
                    pool.wait_ge(a_th, g + 1)
                    nc.gpsimd.tensor_tensor(res[:, j2], x1[:, j], th[:, j2], ALU.add).then_inc(g_res, 1)
                if live(t, -3):
                    g, j2 = t - 3, (k + 1) % 2
                    pool.wait_ge(v_ago, g + 1)
                    nc.gpsimd.tensor_tensor(ve_o[:, j2], ag_o[:, j2, :, 1], eps[:], ALU.add).then_inc(g_eo, 1)
                    nc.gpsimd.tensor_tensor(nm_o[:, j2], ag_o[:, j2, :, 0], minus[:], ALU.mult)
                    pool.wait_ge(g_eo, g + 1)
                    nc.gpsimd.tensor_tensor(rs_o[:, j2], ve_o[:, j2], half_pow[:, 2:4], ALU.pow).then_inc(g_ro, 1)
                    pool.wait_ge(g_ro, g + 1)
                    nc.gpsimd.tensor_tensor(nb_o[:, j2], nm_o[:, j2], rs_o[:, j2], ALU.mult).then_inc(g_nbo, 1)
                if live(t, 3):
                    g, j2 = t + 3, (k + 1) % 2
                    pool.wait_ge(a_ht, g + 1)
                    nc.gpsimd.tensor_tensor(cnt1[:, j2], cnt[:, j2], tiny[:], ALU.add).then_inc(g_cnt, 1)
                    pool.wait_ge(g_cnt, g + 1)
                    nc.gpsimd.tensor_tensor(Be[:, j2], cnt1[:, j2], half_pow[:, 0:CT], ALU.pow).then_inc(g_be, 1)
                    pool.wait_ge(g_be, g + 1)
                    nc.gpsimd.tensor_tensor(Behi[:, j2], Be[:, j2], ones_sq[:, 0:CT], ALU.mult).then_inc(g_behi, 1)

            run_slots(pool, slot)

        @block.scalar
        def _(act):
            def w1_high():
                act.wait_ge(w1_ps, 1)
                nc.scalar.copy(W1hi[:], ps[:, G_BANK[0]:G_BANK[0] + 2, 0:DH]).then_inc(w1_hi, 1)

            def g_w_high():
                act.wait_ge(s_wb, 4 * 16)
                nc.scalar.copy(Whi[:], Wn[:]).then_inc(ww_hi, 1)
                act.wait_ge(g_ps, 1)
                nc.scalar.copy(Ghi[:].rearrange("p t c -> p (t c)"), ps[:, G_BANK[0]:G_BANK[0] + 2].rearrange(
                    "p t c -> p (t c)")).then_inc(gg_hi, 1)
                act.wait_ge(b_ps, 1)
                nc.scalar.copy(bW_b[:], ps[:, B_BANK, 0:D]).then_inc(bw_in, 1)

            def slot(t, k):
                if live(t, -1):
                    g, j, j2 = t - 1, (k + 3) % 4, (k + 1) % 2
                    act.wait_ge(a_x1, g + 1)
                    for c in range(CT):
                        last = nc.scalar.activation(xdhi[:, j2, c], x1[:, j, c], ACT.Copy, scale=sc[:, j, 2 + c:3 + c])
                    last.then_inc(a_xd, 1)
                if live(t, 0):
                    g, j2 = t, k % 2
                    act.wait_ge(v_w, g + 1)
                    nc.scalar.copy(hwhi[:, j2], hw[:, j2]).then_inc(a_w, 1)
                if live(t, 2):
                    g, j = t + 2, (k + 2) % 4
                    act.wait_ge(p_s, g + 1)
                    nc.scalar.copy(Shi[:, j], ps[:, S_BANK[0]:S_BANK[0] + 2, 0:C]).then_inc(a_s, 1)
                if live(t, -2):
                    g, j2 = t - 2, k % 2
                    act.wait_ge(v_a, g + 1)
                    nc.scalar.activation(th[:, j2], a_pre[:, j2], ACT.Tanh).then_inc(a_th, 1)
                if live(t, 1):
                    g, j2 = t + 1, (k + 1) % 2
                    act.wait_ge(v_z1, g + 1)
                    nc.scalar.activation(v[:, j2, 1], z[:, j2, 1], ACT.Relu).then_inc(a_relu1, 1)
                if live(t, -1):
                    g, j2 = t - 1, (k + 1) % 2
                    act.wait_ge(p_z, g + 1)
                    nc.scalar.copy(zhi[:, j2].rearrange("p t c -> p (t c)"), ps[:, Z_BANK]).then_inc(a_z, 1)
                once(t, -1, g_w_high)
                if live(t, 1):
                    g, j2 = t + 1, (k + 1) % 2
                    act.wait_ge(v_z0, g + 1)
                    nc.scalar.activation(v[:, j2, 0], z[:, j2, 0], ACT.Relu).then_inc(a_relu0, 1)
                if live(t, 3):
                    g, j, j2 = t + 3, (k + 3) % 4, (k + 1) % 2
                    act.wait_ge(p_ht, g + 1)
                    for e in range(CT):
                        last = nc.scalar.activation(HT[:, j, e], psHT[:, e * C:(e + 1) * C], ACT.Copy,
                                                    accum_out=cnt[:, j2, e:e + 1])
                    last.then_inc(a_ht, 1)
                if live(t, 1):
                    g, j2 = t + 1, (k + 1) % 2
                    act.wait_ge(p_v0, g + 1)
                    nc.scalar.copy(vhi[:, j2, 0:2].rearrange("p t c -> p (t c)"), ps[:, V_BANK[0]]).then_inc(a_v0, 1)
                if live(t, 1):
                    g, j2 = t + 1, (k + 1) % 2
                    act.wait_ge(p_v1, g + 1)
                    nc.scalar.copy(vhi[:, j2, 2:4].rearrange("p t c -> p (t c)"), ps[:, V_BANK[1]]).then_inc(a_v1, 1)
                if live(t, 3):
                    g, j, j2 = t + 3, (k + 3) % 4, (k + 1) % 2
                    act.wait_ge(s_x[j], loaded(g, j))
                    nc.scalar.copy(xhi[:, j2], x_t[:, j]).then_inc(a_x, 1)
                once(t, -2, w1_high)
                if live(t, 3):
                    g, j, j2 = t + 3, (k + 3) % 4, (k + 1) % 2
                    act.wait_ge(g_behi, g + 1)
                    for e in range(CT):
                        last = nc.scalar.activation(HBhi[:, j2, e, 0:C], HT[:, j, e].bitcast(F32), ACT.Copy,
                                                    scale=Behi[:, j2, e:e + 1].bitcast(F32))
                    last.then_inc(a_hb, 1)
                if live(t, 2):
                    g, j2 = t + 2, k % 2
                    act.wait_ge(p_u, g + 1)
                    nc.scalar.copy(uhi[:, j2].rearrange("p t c -> p (t c)"), ps[:, U_BANK]).then_inc(a_u, 1)
                if live(t, -3):
                    g, j2 = t - 3, (k + 1) % 2
                    act.wait_ge(g_nbo, g + 1)
                    if live(g, -2):
                        act.wait_ge(s_out[j2], (g - j2) * 8)
                    for c in range(CT):
                        last = nc.scalar.activation(out_t[:, j2, c], res[:, j2, c], ACT.Identity,
                                                    bias=nb_o[:, j2, c:c + 1], scale=rs_o[:, j2, c:c + 1])
                    last.then_inc(a_o, 1)
                if live(t, 0):
                    g, j, j2 = t, k, k % 2
                    act.wait_ge(g_nby, g + 1)
                    for c in range(CT):
                        last = nc.scalar.activation(x1[:, j, c], y[:, j2, c], ACT.Identity, bias=nb_y[:, j2, c:c + 1],
                                                    scale=rs_y[:, j2, c:c + 1])
                    last.then_inc(a_x1, 1)

            run_slots(act, slot)

        @block.vector
        def _(dve):
            def gamma_beta_products():
                dve.wait_ge(s_w2, 3 * 16)
                for m, vec, total in ((Gn, gamma_b, g_sum), (Bn, beta_b, b_sum)):
                    for o in range(DT):
                        last = nc.vector.scalar_tensor_tensor(m[:, o], W2n[:, o], 1.0, vec, ALU.mult, ALU.mult,
                                                              accum_out=total[:, o:o + 1])
                    last.then_inc(gb_n, 1)

            def wait_biases():
                dve.wait_ge(s_wb, 4 * 16)

            def w1_low():
                dve.wait_ge(w1_hi, 1)
                nc.vector.tensor_tensor(W1lo[:], ps[:, G_BANK[0]:G_BANK[0] + 2, 0:DH], W1hi[:].bitcast(F32),
                                        ALU.subtract).then_inc(w1_lo, 1)

            def centre_g():
                dve.wait_ge(gb_n, 1)
                nc.vector.tensor_scalar(g_mean[:], g_sum[:], 1.0 / DH, None, ALU.mult).then_inc(gm_ready, 1)
                dve.wait_ge(gb_n, 2)
                dve.wait_ge(gm_ready, 1)
                for o in range(DT):
                    nc.vector.tensor_scalar(Gn[:, o], Gn[:, o], g_mean[:, o:o + 1], None, ALU.subtract).then_inc(g_c, 1)
                dve.wait_ge(s_id, 10)
                for o in range(DT):
                    last = nc.vector.tensor_scalar(b_sq[:, o], ones_sq[:], b_sum[:, o:o + 1], None, ALU.mult)
                last.then_inc(b_c, 1)

            def g_w_low():
                dve.wait_ge(ww_hi, 1)
                nc.vector.tensor_tensor(Wlo[:], Wn[:], Whi[:].bitcast(F32), ALU.subtract).then_inc(ww_lo, 1)
                dve.wait_ge(gg_hi, 1)
                nc.vector.tensor_tensor(Glo[:].rearrange("p t c -> p (t c)"), ps[:, G_BANK[0]:G_BANK[0] + 2].rearrange(
                    "p t c -> p (t c)"), Ghi[:].rearrange("p t c -> p (t c)").bitcast(F32), ALU.subtract).then_inc(gg_lo, 1)
                dve.wait_ge(bw_in, 1)

            def slot(t, k):
                if live(t, -2):
                    g, j2 = t - 2, k % 2
                    dve.wait_ge(a_z, g + 1)
                    nc.vector.tensor_tensor(zlo[:, j2].rearrange("p t c -> p (t c)"), ps[:, Z_BANK],
                                            zhi[:, j2].rearrange("p t c -> p (t c)").bitcast(F32),
                                            ALU.subtract).then_inc(v_z, 1)
                if live(t, -1):
                    g, j, j2 = t - 1, (k + 3) % 4, (k + 1) % 2
                    dve.wait_ge(p_y, g + 1)
                    for c in range(CT):
                        last = nc.vector.scalar_tensor_tensor(y[:, j2, c], ps[:, Y_BANK, c * D:(c + 1) * D],
                                                              Dn[:, j, c:c + 1], xb[:, j2, c], ALU.mult, ALU.add)
                    last.then_inc(v_y, 1)
                if live(t, 1):
                    g, j, j2 = t + 1, (k + 1) % 4, (k + 1) % 2
                    d_col = ps[:, S_BANK[0]:S_BANK[0] + 2, C]
                    rc_col = ps[:, S_BANK[0]:S_BANK[0] + 2, C + 1]
                    nc.vector.tensor_scalar(sc_in[:, j2, 0:2], d_col, TINY, None, ALU.max)
                    nc.vector.tensor_scalar(sc_mask[:, j2], d_col, 0.0, None, ALU.is_gt)
                    nc.vector.scalar_tensor_tensor(sc_in[:, j2, 2:4], wd_t[:, j, 1], 0.0, rc_col,
                                                   ALU.is_equal, ALU.add).then_inc(v_sc, 1)
                if live(t, -1):
                    g, j2 = t - 1, (k + 1) % 2
                    dve.wait_ge(v_y, g + 1)
                    for c in range(CT):
                        last = nc.vector.bn_stats(bn_y[:, j2, c], y[:, j2, c])
                    last.then_inc(v_bny, 1)
                once(t, 0, g_w_low)
                if live(t, 0):
                    g, j2 = t, k % 2
                    dve.wait_ge(a_v0, g + 1)
                    nc.vector.tensor_tensor(vlo[:, j2, 0:2].rearrange("p t c -> p (t c)"), ps[:, V_BANK[0]],
                                            vhi[:, j2, 0:2].rearrange("p t c -> p (t c)").bitcast(F32),
                                            ALU.subtract).then_inc(v_v0, 1)
                if live(t, 0):
                    g, j2 = t, k % 2
                    dve.wait_ge(a_v1, g + 1)
                    if live(t, -1):
                        dve.wait_ge(v_bny, t)
                    nc.vector.tensor_tensor(vlo[:, j2, 2:4].rearrange("p t c -> p (t c)"), ps[:, V_BANK[1]],
                                            vhi[:, j2, 2:4].rearrange("p t c -> p (t c)").bitcast(F32),
                                            ALU.subtract).then_inc(v_v1, 1)
                if live(t, -1):
                    g, j2 = t - 1, (k + 1) % 2
                    if not live(t, 0):
                        dve.wait_ge(v_bny, g + 1)
                    for c in range(CT):
                        last = nc.vector.bn_aggr(ag_y[:, j2, c], bn_y[:, j2, c])
                    last.then_inc(v_agy, 1)
                if live(t, 0):
                    g, j2 = t, k % 2
                    nc.vector.bn_stats(bn_v[:, j2, 0], v[:, j2, 0]).then_inc(v_bnv0, 1)
                if live(t, 0):
                    g, j, j2 = t, k, k % 2
                    nc.vector.scalar_tensor_tensor(xb[:, j2], x_t[:, j], 2.0, b2_b[:], ALU.mult, ALU.add).then_inc(v_xb, 1)
                once(t, -1, gamma_beta_products)
                if live(t, 3):
                    g, j, j2 = t + 3, (k + 3) % 4, (k + 1) % 2
                    dve.wait_ge(s_adj[j], loaded(g, j))
                    if live(t, 0):
                        dve.wait_ge(v_bnv0, t + 1)
                    nc.vector.tensor_scalar(Hb[:, j2], adj_t[:, j], 0.0, None, ALU.not_equal).then_inc(v_h, 1)
                if live(t, 0):
                    g, j2 = t, k % 2
                    if not live(t, 3):
                        dve.wait_ge(v_bnv0, g + 1)
                    for c in range(CT):
                        last = nc.vector.bn_aggr(ag_v[:, j2, c], bn_v[:, j2, c])
                    last.then_inc(v_agv, 1)
                if live(t, -3):
                    g, j2 = t - 3, (k + 1) % 2
                    dve.wait_ge(g_res, g + 1)
                    for c in range(CT):
                        last = nc.vector.bn_stats(bn_o[:, j2, c], res[:, j2, c])
                    last.then_inc(v_bno, 1)
                once(t, -1, w1_low)
                if live(t, 1):
                    g, j2 = t + 1, (k + 1) % 2
                    dve.wait_ge(a_u, g + 1)
                    nc.vector.tensor_tensor(ulo[:, j2].rearrange("p t c -> p (t c)"), ps[:, U_BANK],
                                            uhi[:, j2].rearrange("p t c -> p (t c)").bitcast(F32),
                                            ALU.subtract).then_inc(v_u, 1)
                if live(t, -2):
                    g, j, j2 = t - 2, (k + 2) % 4, k % 2
                    dve.wait_ge(p_a, g + 1)
                    for c in range(CT):
                        last = nc.vector.scalar_tensor_tensor(a_pre[:, j2, c], ps[:, A_BANK, c * D:(c + 1) * D],
                                                              sc[:, j, 2 + c:3 + c], bL_b[:], ALU.mult, ALU.add)
                    last.then_inc(v_a, 1)
                if live(t, 0):
                    g, j2 = t, k % 2
                    dve.wait_ge(p_w, g + 1)
                    dve.wait_ge(g_rv, g + 1)
                    for c in range(CT):
                        last = nc.vector.scalar_tensor_tensor(hw[:, j2, c], ps[:, W_BANK, c * D:(c + 1) * D],
                                                              rs_v[:, j2, c:c + 1], bW_b[:], ALU.mult, ALU.add)
                    last.then_inc(v_w, 1)
                once(t, -1, centre_g)
                if live(t, 2):
                    g, j = t + 2, (k + 2) % 4
                    dve.wait_ge(p_s, g + 1)
                    nc.vector.tensor_tensor(diag_blocks(HT[:, j]), diag_blocks(HT[:, j]).bitcast(F32),
                                            ident[:].unsqueeze(1).to_broadcast([P, CT, P]), ALU.max).then_inc(v_at, 1)
                if live(t, -1):
                    g, j, j2 = t - 1, (k + 3) % 4, (k + 1) % 2
                    dve.wait_ge(a_xd, g + 1)
                    for c in range(CT):
                        last = nc.vector.scalar_tensor_tensor(xdlo[:, j2, c], x1[:, j, c], sc[:, j, 2 + c:3 + c],
                                                              xdhi[:, j2, c].bitcast(F32), ALU.mult, ALU.subtract)
                    last.then_inc(v_xd, 1)
                once(t, -1, wait_biases)
                if live(t, 1):
                    g, j, j2 = t + 1, (k + 1) % 4, (k + 1) % 2
                    dve.wait_ge(p_r1, g + 1)
                    dve.wait_ge(g_dn, g + 1)
                    nc.vector.scalar_tensor_tensor(z[:, j2, 1], ps[:, R_BANK[1], 0:DH], Dn[:, j, 1:2],
                                                   b1_b[:], ALU.mult, ALU.add).then_inc(v_z1, 1)
                if live(t, 2):
                    g, j = t + 2, (k + 2) % 4
                    dve.wait_ge(a_s, g + 1)
                    nc.vector.tensor_tensor(Slo[:, j], ps[:, S_BANK[0]:S_BANK[0] + 2, 0:C], Shi[:, j].bitcast(F32),
                                            ALU.subtract).then_inc(v_s, 1)
                if live(t, 1):
                    g, j, j2 = t + 1, (k + 1) % 4, (k + 1) % 2
                    dve.wait_ge(p_r0, g + 1)
                    if live(t, -3):
                        dve.wait_ge(v_bno, t - 2)
                    nc.vector.scalar_tensor_tensor(z[:, j2, 0], ps[:, R_BANK[0], 0:DH], Dn[:, j, 0:1],
                                                   b1_b[:], ALU.mult, ALU.add).then_inc(v_z0, 1)
                if live(t, -3):
                    g, j2 = t - 3, (k + 1) % 2
                    if not live(t, 1):
                        dve.wait_ge(v_bno, g + 1)
                    for c in range(CT):
                        last = nc.vector.bn_aggr(ag_o[:, j2, c], bn_o[:, j2, c])
                    last.then_inc(v_ago, 1)
                if live(t, 1):
                    g, j2 = t + 1, (k + 1) % 2
                    dve.wait_ge(a_relu1, g + 1)
                    nc.vector.bn_stats(bn_v[:, j2, 1], v[:, j2, 1]).then_inc(v_bnv1, 1)

            run_slots(dve, slot)

        @block.tensor
        def _(pe):
            def product(out_ap, pairs, kt):
                n, total = 0, len(pairs) * kt
                for left, right in pairs:
                    for q in range(kt):
                        last = nc.tensor.matmul(out_ap, left(q), right(q), start=(n == 0), stop=(n == total - 1))
                        n += 1
                return last

            def three(lhi, llo, rhi, rlo):
                return [(lhi, rhi), (lhi, rlo), (llo, rhi)]

            def wait_constants():
                pe.wait_ge(s_id, 10)

            def transpose_w1():
                pe.wait_ge(s_w1, 16)
                for d in range(DT):
                    for h in range(HT_):
                        last = nc.tensor.transpose(ps[:, G_BANK[d], h * P:(h + 1) * P], W1n[:, h, d * P:(d + 1) * P],
                                                   ident[:])
                last.then_inc(w1_ps, 1)

            def transpose_g():
                pe.wait_ge(g_c, 2)
                for h in range(HT_):
                    for o in range(DT):
                        q = (h % 2) * D + o * P
                        last = nc.tensor.transpose(ps[:, G_BANK[h // 2], q:q + P], Gn[:, o, h * P:(h + 1) * P], ident[:])
                last.then_inc(g_ps, 1)
                pe.wait_ge(b_c, 1)
                for o in range(DT):
                    last = nc.tensor.matmul(ps[:, B_BANK, o * P:(o + 1) * P], b_sq[:, o], ident[:], start=True, stop=True)
                last.then_inc(b_ps, 1)

            def wait_w1():
                pe.wait_ge(w1_lo, 1)

            def wait_g():
                pe.wait_ge(gg_lo, 1)
                pe.wait_ge(bw_in, 1)
                pe.wait_ge(ww_lo, 1)

            def slot(t, k):
                once(t, 1, wait_w1)
                if live(t, -1):
                    g, j2 = t - 1, (k + 1) % 2
                    pe.wait_ge(v_u, g + 1)
                    product(ps[:, R_BANK[1], 0:DH],
                            three(lambda q: uhi[:, j2, q, P:2 * P], lambda q: ulo[:, j2, q, P:2 * P],
                                  lambda q: W1hi[:, q], lambda q: W1lo[:, q]), DT).then_inc(p_r1, 1)
                once(t, 1, transpose_g)
                if live(t, -1):
                    g, j2 = t - 1, (k + 1) % 2
                    product(ps[:, R_BANK[0], 0:DH],
                            three(lambda q: uhi[:, j2, q, 0:P], lambda q: ulo[:, j2, q, 0:P],
                                  lambda q: W1hi[:, q], lambda q: W1lo[:, q]), DT).then_inc(p_r0, 1)
                if live(t, -3):
                    g, j, j2 = t - 3, (k + 1) % 4, (k + 1) % 2
                    pe.wait_ge(v_xd, g + 1)
                    for d in range(DT):
                        cs = slice(d * P, (d + 1) * P)
                        last = product(ps[:, Z_BANK, d * C:(d + 1) * C],
                                       [(lambda q: xdhi[:, j2, q, cs], lambda q: HT[:, j, q]),
                                        (lambda q: xdlo[:, j2, q, cs], lambda q: HT[:, j, q])], CT)
                    last.then_inc(p_z, 1)
                if live(t, -2):
                    g, j, j2 = t - 2, (k + 2) % 4, k % 2
                    pe.wait_ge(g_w, g + 1)
                    for c in range(CT):
                        cs = slice(c * P, (c + 1) * P)
                        last = product(ps[:, Y_BANK, c * D:(c + 1) * D],
                                       three(lambda q: Shi[:, j, q, cs], lambda q: Slo[:, j, q, cs],
                                             lambda q: hwhi[:, j2, q], lambda q: hwlo[:, j2, q]), CT)
                    last.then_inc(p_y, 1)
                once(t, -1, wait_constants)
                if live(t, 1):
                    g, j2 = t + 1, (k + 1) % 2
                    pe.wait_ge(v_h, g + 1)
                    if live(g, -2):
                        pe.wait_ge(v_z1, g - 1)
                    elif live(g, -2):
                        pe.wait_ge(v_u, g - 1)
                    elif live(g, -1):
                        pe.wait_ge(a_ht, g)
                    for e in range(CT):
                        for c in range(CT):
                            last = nc.tensor.transpose(psHT[:, e * C + c * P:e * C + (c + 1) * P],
                                                       Hb[:, j2, c, e * P:(e + 1) * P], ident_bf[:])
                    last.then_inc(p_ht, 1)
                if live(t, -1):
                    g, j2 = t - 1, (k + 1) % 2
                    pe.wait_ge(a_relu0, g + 1)
                    for h in range(2):
                        for c in range(CT):
                            last = nc.tensor.transpose(ps[:, V_BANK[0], h * C + c * P:h * C + (c + 1) * P],
                                                       v[:, j2, c, h * P:(h + 1) * P], ident[:])
                    last.then_inc(p_v0, 1)
                if live(t, -1):
                    g, j2 = t - 1, (k + 1) % 2
                    for h in range(2):
                        for c in range(CT):
                            last = nc.tensor.transpose(ps[:, V_BANK[1], h * C + c * P:h * C + (c + 1) * P],
                                                       v[:, j2, c, (h + 2) * P:(h + 3) * P], ident[:])
                    last.then_inc(p_v1, 1)
                if live(t, -3):
                    g, j2 = t - 3, (k + 1) % 2
                    pe.wait_ge(v_z, g + 1)
                    for c in range(CT):
                        cs = slice(c * P, (c + 1) * P)
                        last = product(ps[:, A_BANK, c * D:(c + 1) * D],
                                       three(lambda q: zhi[:, j2, q, cs], lambda q: zlo[:, j2, q, cs],
                                             lambda q: Whi[:, q], lambda q: Wlo[:, q]), DT)
                    last.then_inc(p_a, 1)
                once(t, 0, transpose_w1)
                if live(t, 0):
                    g, j, j2 = t, k, k % 2
                    pe.wait_ge(g_x, g + 1)
                    pe.wait_ge(v_s, g + 1)
                    if live(g, 1):
                        pe.wait_ge(a_ht, g + 2)
                    elif live(g, -1):
                        pe.wait_ge(v_z1, g)
                    elif live(g, -1):
                        pe.wait_ge(v_u, g)
                    for d in range(DT):
                        cs = slice(d * P, (d + 1) * P)
                        last = product(ps[:, U_BANK, d * C:(d + 1) * C],
                                       three(lambda q: xhi[:, j2, q, cs], lambda q: xlo[:, j2, q, cs],
                                             lambda q: Shi[:, j, q], lambda q: Slo[:, j, q]), CT)
                    last.then_inc(p_u, 1)
                once(t, 1, wait_g)
                if live(t, -1):
                    g, j2 = t - 1, (k + 1) % 2
                    pe.wait_ge(v_v1, g + 1)
                    for c in range(CT):
                        cs = slice(c * P, (c + 1) * P)
                        last = product(ps[:, W_BANK, c * D:(c + 1) * D],
                                       three(lambda q: vhi[:, j2, q, cs], lambda q: vlo[:, j2, q, cs],
                                             lambda q: Ghi[:, q], lambda q: Glo[:, q]), HT_)
                    last.then_inc(p_w, 1)
                if live(t, 1):
                    g, j, j2 = t + 1, (k + 1) % 4, (k + 1) % 2
                    pe.wait_ge(a_hb, g + 1)
                    pe.wait_ge(g_hb, g + 1)
                    if live(g, -1):
                        pe.wait_ge(v_sc, g)
                    for c in range(CT):
                        cs = slice(c * P, (c + 1) * P)
                        last = product(ps[:, S_BANK[c], 0:C + 2],
                                       [(lambda q: HT[:, j, q, cs], lambda q: HBhi[:, j2, q]),
                                        (lambda q: HT[:, j, q, cs], lambda q: HBlo[:, j2, q])], CT)
                    last.then_inc(p_s, 1)

            run_slots(pe, slot)


_INS = ['x', 'adj', 'L0_gnn_W1', 'L0_gnn_b1', 'L0_gnn_gamma', 'L0_gnn_beta', 'L0_gnn_W2', 'L0_gnn_b2',
        'L1_gnn_W', 'L1_gnn_b']


def kernel(**inputs):
    import numpy as _np
    import concourse.bacc as _bacc
    from concourse import mybir as _mybir
    from concourse.bass_utils import run_bass_kernel_spmd as _run

    nc = _bacc.Bacc("TRN2", target_bir_lowering=False, num_devices=1)
    arrays, args = {}, []
    for name in _INS:
        a = _np.ascontiguousarray(inputs[name])
        arrays[f"in_{name}_dram"] = a
        args.append(nc.dram_tensor(f"in_{name}_dram", a.shape, _mybir.dt.from_np(a.dtype), kind="ExternalInput").ap())
    shape = arrays["in_x_dram"].shape
    out = nc.dram_tensor("out_0_dram", shape, _mybir.dt.from_np(_np.dtype("float32")), kind="ExternalOutput").ap()
    bass_resnorm_graph_layers(nc, *args, out)
    r = _run(nc, [arrays], core_ids=[0])
    return r.results[0]["out_0_dram"]
```
